# Optimizing a Trainium2 kernel written in Bass

```python
import numpy as np
import jax
import jax.numpy as jnp

def _softmax(x, axis=-1):
    return jax.nn.softmax(x, axis=axis)

def _gelu(x):
    return jax.nn.gelu(x, approximate=True)

def _silu(x):
    return jax.nn.silu(x)

def _sigmoid(x):
    return jax.nn.sigmoid(x)

def _layernorm(x, axis=-1, eps=1e-05):
    m = jnp.mean(x, axis=axis, keepdims=True)
    v = jnp.var(x, axis=axis, keepdims=True)
    return (x - m) / jnp.sqrt(v + eps)

def _scatter_add(tgt, idx, src, axis=0):
    return tgt.at[idx].add(src)

def _segment_sum(src, seg, n):
    return jax.ops.segment_sum(src, seg, n)
kernel_name = 'mk_adaln_d1_jaxref_r2_91ada3'

def setup_inputs(seed: int=0):
    np.random.seed(seed)
    _w = jnp.asarray

    def _L0_attn_setup():
        import jax, jax.numpy as jnp
        import numpy as np
        D_MODEL = 512
        N_HEADS = 16
        HEAD_DIM = D_MODEL // N_HEADS
        WINDOW = 128

        def _window_starts(seq_len, window):
            starts = []
            for i in range(0, seq_len, window // 2):
                end = min(i + window, seq_len)
                starts.append(max(0, end - window))
                if end == seq_len:
                    break
            return np.asarray(starts, dtype=np.int32)
        key = jax.random.key(seed)
        ks = jax.random.split(key, 9)
        B, S = (4, 2048)
        sc = 1.0 / np.sqrt(D_MODEL)
        return {'x': jax.random.normal(ks[0], (B, S, D_MODEL), jnp.float32), 'Wq': jax.random.normal(ks[1], (D_MODEL, D_MODEL), jnp.float32) * sc, 'bq': jax.random.normal(ks[2], (D_MODEL,), jnp.float32) * 0.02, 'Wk': jax.random.normal(ks[3], (D_MODEL, D_MODEL), jnp.float32) * sc, 'bk': jax.random.normal(ks[4], (D_MODEL,), jnp.float32) * 0.02, 'Wv': jax.random.normal(ks[5], (D_MODEL, D_MODEL), jnp.float32) * sc, 'bv': jax.random.normal(ks[6], (D_MODEL,), jnp.float32) * 0.02, 'Wo': jax.random.normal(ks[7], (D_MODEL, D_MODEL), jnp.float32) * sc, 'bo': jax.random.normal(ks[8], (D_MODEL,), jnp.float32) * 0.02}
    _L0_attn_in = _L0_attn_setup()

    def _L0_ffn_setup():
        import jax, jax.numpy as jnp
        import numpy as np
        ALPHA = 1.0
        key = jax.random.key(seed)
        ks = jax.random.split(key, 7)
        B, S, IN, OUT = (8, 4096, 512, 512)
        RANK, DDIM, UDIM = (4, 100, 50)
        return {'hidden_states': jax.random.normal(ks[0], (B, S, IN), dtype=jnp.float32), 'W': jax.random.normal(ks[1], (OUT, IN), dtype=jnp.float32) * 0.02, 'b': jax.random.normal(ks[2], (OUT,), dtype=jnp.float32) * 0.02, 'lora_down': jax.random.normal(ks[3], (RANK, DDIM), dtype=jnp.float32) * 0.1, 'lora_up': jax.random.normal(ks[4], (UDIM, RANK), dtype=jnp.float32) * 0.1, 'down_aux': jax.random.normal(ks[5], (DDIM, IN), dtype=jnp.float32) * 0.03, 'up_aux': jax.random.normal(ks[6], (OUT, UDIM), dtype=jnp.float32) * 0.03}
    _L0_ffn_in = _L0_ffn_setup()
    _L0_c = _w((lambda *s: np.random.randn(*s).astype(np.float32) * 0.05)(8, 512))
    _L0_wmod = _w((lambda *s: np.random.randn(*s).astype(np.float32) * 0.05)(512, 6 * 512) * 512 ** (-0.5))
    _d = {'L0_attn_x': _L0_attn_in['x'], 'L0_attn_Wq': _L0_attn_in['Wq'], 'L0_attn_bq': _L0_attn_in['bq'], 'L0_attn_Wk': _L0_attn_in['Wk'], 'L0_attn_bk': _L0_attn_in['bk'], 'L0_attn_Wv': _L0_attn_in['Wv'], 'L0_attn_bv': _L0_attn_in['bv'], 'L0_attn_Wo': _L0_attn_in['Wo'], 'L0_attn_bo': _L0_attn_in['bo'], 'L0_ffn_W': _L0_ffn_in['W'], 'L0_ffn_b': _L0_ffn_in['b'], 'L0_ffn_lora_down': _L0_ffn_in['lora_down'], 'L0_ffn_lora_up': _L0_ffn_in['lora_up'], 'L0_ffn_down_aux': _L0_ffn_in['down_aux'], 'L0_ffn_up_aux': _L0_ffn_in['up_aux'], 'L0_c': _L0_c, 'L0_wmod': _L0_wmod}
    _x0 = _d['L0_attn_x']
    _d['L0_attn_x'] = jax.random.normal(jax.random.fold_in(jax.random.key(seed), 1), (8, 2048, 512), dtype=_x0.dtype)
    del _x0
    return _d

def reference(L0_attn_x, L0_attn_Wq, L0_attn_bq, L0_attn_Wk, L0_attn_bk, L0_attn_Wv, L0_attn_bv, L0_attn_Wo, L0_attn_bo, L0_ffn_W, L0_ffn_b, L0_ffn_lora_down, L0_ffn_lora_up, L0_ffn_down_aux, L0_ffn_up_aux, L0_c, L0_wmod):

    def _L0_attn_ref(x, Wq, bq, Wk, bk, Wv, bv, Wo, bo):
        import jax, jax.numpy as jnp
        import numpy as np
        D_MODEL = 512
        N_HEADS = 16
        HEAD_DIM = D_MODEL // N_HEADS
        WINDOW = 128

        def _window_starts(seq_len, window):
            starts = []
            for i in range(0, seq_len, window // 2):
                end = min(i + window, seq_len)
                starts.append(max(0, end - window))
                if end == seq_len:
                    break
            return np.asarray(starts, dtype=np.int32)
        B, S, D = x.shape
        q = x @ Wq + bq
        k = x @ Wk + bk
        v = x @ Wv + bv
        starts = _window_starts(S, WINDOW)
        idx = starts[:, None] + np.arange(WINDOW)[None, :]
        idx_j = jnp.asarray(idx)
        qw = q[:, idx_j]
        kw = k[:, idx_j]
        vw = v[:, idx_j]
        scores = jnp.einsum('bwqd,bwkd->bwqk', qw, kw) / np.sqrt(HEAD_DIM)
        attn = jax.nn.softmax(scores, axis=-1)
        out_w = jnp.einsum('bwqk,bwkd->bwqd', attn, vw)
        flat_idx = idx.reshape(-1)
        out = jnp.zeros((B, S, D), x.dtype).at[:, flat_idx].add(out_w.reshape(B, -1, D))
        counts = jnp.zeros((S,), x.dtype).at[flat_idx].add(1.0)
        out = out / counts[None, :, None]
        return out @ Wo + bo

    def _L0_ffn_ref(hidden_states, W, b, lora_down, lora_up, down_aux, up_aux):
        import jax, jax.numpy as jnp
        import numpy as np
        ALPHA = 1.0
        lilora_weight = up_aux @ (lora_up @ (lora_down @ down_aux))
        base = jnp.einsum('bsi,oi->bso', hidden_states, W) + b
        delta = jnp.einsum('bsi,oi->bso', hidden_states, lilora_weight)
        return base + ALPHA * delta
    x = L0_attn_x
    mod = (_silu(L0_c) @ L0_wmod).reshape(L0_c.shape[0], 6, 1, -1)
    sa, ca, ga, sb, cb, gb = (mod[:, 0], mod[:, 1], mod[:, 2], mod[:, 3], mod[:, 4], mod[:, 5])
    ga = (2 * (ga >= 0) - 1) * jnp.maximum(jnp.abs(ga), 0.25)
    gb = (2 * (gb >= 0) - 1) * jnp.maximum(jnp.abs(gb), 0.25)
    h = _layernorm(x, axis=-1) * (1 + ca) + sa
    x = x + ga * _L0_attn_ref(h, L0_attn_Wq, L0_attn_bq, L0_attn_Wk, L0_attn_bk, L0_attn_Wv, L0_attn_bv, L0_attn_Wo, L0_attn_bo)
    h = _layernorm(x, axis=-1) * (1 + cb) + sb
    x = x + gb * _L0_ffn_ref(h, L0_ffn_W, L0_ffn_b, L0_ffn_lora_down, L0_ffn_lora_up, L0_ffn_down_aux, L0_ffn_up_aux)
    return x

_drawn_inputs = setup_inputs


def setup_inputs(seed=0):
    import zlib

    import numpy as np

    out = dict(_drawn_inputs(seed))
    spreads = {}
    factors = {'L0_attn_bq': 8.0,
     'L0_attn_bk': 200.0,
     'L0_attn_bv': 8.0,
     'L0_attn_bo': 8.0,
     'L0_ffn_b': 200.0,
     'L0_ffn_lora_down': 8.0,
     'L0_ffn_lora_up': 8.0,
     'L0_ffn_down_aux': 8.0,
     'L0_ffn_up_aux': 8.0,
     'L0_ffn_W': 8.0}
    for name, (base, spread) in spreads.items():
        noise = np.random.default_rng([zlib.crc32(name.encode()), seed]).standard_normal(out[name].shape)
        drawn = base * np.exp(spread * noise) if base else spread * noise
        out[name] = jnp.asarray(drawn.astype(out[name].dtype))
    for name, factor in factors.items():
        out[name] = (out[name] * factor).astype(out[name].dtype)
    return out
```

```python
from contextlib import ExitStack

import concourse.bass as bass
from concourse import mybir

ALU = mybir.AluOpType
ACT = mybir.ActivationFunctionType
AX_X = mybir.AxisListType.X
F32 = mybir.dt.float32
F32R = mybir.dt.float32r
HI, LO = 0, 1

P = 128
HALF = P // 2
HEAD_DIM = 32
LN_EPS = 1e-5
GATE_MIN = 0.25

RING = 8
GROUP = 4
XRING = 16


def adaln_block_kernel(nc, x, Wq, bq, Wk, bk, Wv, bv, Wo, bo, W, b, lora_down, lora_up, down_aux, up_aux,
                       c, wmod, out):
    B, S, D = x.shape
    CH = D // P
    TPB = S // P
    N = B * TPB
    RANK, DDIM = lora_down.shape
    UDIM = lora_up.shape[0]
    KINDS = wmod.shape[1] // D
    SA, CA, GA, SB, CB, GB = range(KINDS)
    SCALE = float(HEAD_DIM) ** -0.5
    ZW = D + 1
    assert TPB == XRING and TPB % RING == 0 and RING == 2 * GROUP and CH * P == D

    x_t = x.rearrange("b (t p) d -> (b t) p d", p=P)
    out_t = out.rearrange("b (t p) d -> (b t) p d", p=P)

    with ExitStack() as ctx:
        def sb(name, shape, dt=F32, stack=ctx):
            return stack.enter_context(nc.sbuf_tensor(name, shape, dt))

        def sem(name):
            return ctx.enter_context(nc.semaphore(name))

        bank_u, bank_v, bank_s, bank_t1, bank_t2, bank_y, bank_o, bank_x = [
            ctx.enter_context(nc.psum_tensor(f"bank_{n}", [P, 512], F32))
            for n in ("u", "v", "s", "t1", "t2", "y", "o", "x")]

        ident = sb("ident", [P, P])
        m_w = sb("m_w", [P, 2, CH, D], F32R)
        vo_w = sb("vo_w", [P, 2, CH, D], F32R)
        ff_w = sb("ff_w", [P, 2, CH, D], F32R)
        u_bias = sb("u_bias", [P, CH])
        cols = sb("cols", [P, B * 4 * CH])
        z_rows = nc.dram_tensor("z_rows", [B, ZW], F32, kind="Internal").ap()
        ga_rows = nc.dram_tensor("ga_rows", [B, D], F32, kind="Internal").ap()
        gb_rows = nc.dram_tensor("gb_rows", [B, D], F32, kind="Internal").ap()
        r1_rows = nc.dram_tensor("r1_rows", [B, D], F32, kind="Internal").ap()
        r2_rows = nc.dram_tensor("r2_rows", [B, D], F32, kind="Internal").ap()

        prepare(nc, locals(), sem)

        main = ExitStack()
        with main:
            ms = lambda name, shape, dt=F32: sb(name, shape, dt, main)
            hT = ms("hT", [P, 2, CH, HALF + RING * P + HALF], F32R)
            uT = ms("uT", [P, 2, 2, CH, GROUP * P], F32R)
            v_sb = ms("v_sb", [P, 2, 2, D], F32R)
            pT = ms("pT", [P, 2, 2 * P], F32R)
            h2T = ms("h2T", [P, 2, 2, CH, P], F32R)
            x_sb = ms("x_sb", [P, XRING, D])
            n1 = ms("n1", [P, D])
            n2 = ms("n2", [P, D])
            h1 = ms("h1", [P, CH, P])
            h2 = ms("h2", [P, CH, P])
            exp_a = ms("exp_a", [P, 2 * P])
            exp_b = ms("exp_b", [P, 2 * P])
            prob_a = ms("prob_a", [P, 2 * P])
            prob = ms("prob", [P, 2 * P])
            gated_y = ms("gated_y", [P, D])
            gated_o = ms("gated_o", [P, D])
            junk = ms("junk", [P, D])
            z_row = ms("z_row", [P, ZW])
            ga_row = ms("ga_row", [P, D])
            gb_row = ms("gb_row", [P, D])
            r1_row = ms("r1_row", [P, D])
            r2_row = ms("r2_row", [P, D])
            cols1 = ms("cols1", [P, 2 * CH])
            cols2 = ms("cols2", [P, 2 * CH])
            stats1 = ms("stats1", [P, 6])
            stats2 = ms("stats2", [P, 6])
            mv1 = ms("mv1", [P, 2])
            mv2 = ms("mv2", [P, 2])
            ve1 = ms("ve1", [P, 1])
            ve2 = ms("ve2", [P, 1])
            rstd1 = ms("rstd1", [P, 1])
            rstd2 = ms("rstd2", [P, 1])
            minus_half = ms("minus_half", [P, 1])
            spare = ms("spare", [P, 1])
            kap = ms("kap", [P, XRING])
            kap_s = ms("kap_s", [P, XRING])
            blk_max = ms("blk_max", [P, 4])
            win_max = ms("win_max", [P, 3])
            max_k = ms("max_k", [P, 3])
            neg_max = ms("neg_max", [P, 3])
            sums = ms("sums", [P, 2])
            recips = ms("recips", [P, 2])
            weights = ms("weights", [P, 2])
            share = ms("share", [P, 3, 2])
            run(nc, locals(), sem)


def prepare(nc, env, sem):
    g = env
    B, D, CH, KINDS, ZW, RANK, DDIM, UDIM = (g[k] for k in ("B", "D", "CH", "KINDS", "ZW", "RANK", "DDIM", "UDIM"))
    SA, CA, GA, SB, CB, GB = range(KINDS)
    ident, m_w, vo_w, ff_w, u_bias, cols = (g[k] for k in ("ident", "m_w", "vo_w", "ff_w", "u_bias", "cols"))
    banks = [g[k] for k in ("bank_u", "bank_v", "bank_s", "bank_t1", "bank_t2", "bank_y", "bank_o", "bank_x")]
    NBANK = len(banks)

    with ExitStack() as ctx:
        def sb(name, shape, dt=F32):
            return ctx.enter_context(nc.sbuf_tensor(name, shape, dt))

        wq_sb, wk_sb, wv_sb, wo_sb, w_sb = [sb(f"{n}_sb", [P, CH, D]) for n in ("wq", "wk", "wv", "wo", "w")]
        wqT, wkT, wvT = [sb(f"{n}T", [P, CH, D]) for n in ("wq", "wk", "wv")]
        wmod_sb = sb("wmod_sb", [P, CH, KINDS * D // 2])
        c_sb = sb("c_sb", [B, D])
        silu_e = sb("silu_e", [B, D])
        silu_d = sb("silu_d", [B, D])
        silu_r = sb("silu_r", [B, D])
        silu_c = sb("silu_c", [B, D])
        scT = sb("scT", [P, CH * B])
        up_sb = sb("up_sb", [P, CH, P])
        upT = sb("upT", [P, D])
        down_sb = sb("down_sb", [DDIM, D])
        ldT = sb("ldT", [DDIM, RANK])
        luT = sb("luT", [RANK, UDIM])
        t1_sb = sb("t1_sb", [RANK, D])
        t2_sb = sb("t2_sb", [UDIM, D])
        bq_col = sb("bq_col", [P, CH])
        bk_col = sb("bk_col", [P, CH])
        bv_col = sb("bv_col", [P, CH])
        bk_rep = sb("bk_rep", [P, CH, B])
        bv_rep = sb("bv_rep", [P, CH, B])
        bq_r, bk_r, bo_r, b_r = [sb(f"{n}_r", [B, D]) for n in ("bq", "bk", "bo", "bff")]
        wqbk = sb("wqbk", [B, D])
        bvo = sb("bvo", [B, D])
        mod = sb("mod", [B, KINDS, D])
        gate = sb("gate", [B, 2, D])
        sign = sb("sign", [B, 2, D])
        size = sb("size", [B, 2, D])
        magn = sb("magn", [B, 2, D])
        z = sb("z", [B, ZW])
        prod = sb("prod", [B, D])
        bqbk = sb("bqbk", [B, 1])
        r1 = sb("r1", [B, D])
        r2 = sb("r2", [B, D])

        in_qk, in_vo, in_w, in_small, in_c, in_mod0, in_mod1 = [
            sem(f"in_{n}") for n in ("qk", "vo", "w", "small", "c", "mod0", "mod1")]
        up_zero, id_zero, id_made = sem("up_zero"), sem("id_zero"), sem("id_made")
        e_made, silu_step, made = sem("e_made"), sem("silu_step"), sem("made")
        hi_made, taken, reps, row_step = sem("hi_made"), sem("taken"), sem("reps"), sem("row_step")
        rows_out = sem("rows_out")

        order = ([("wqT", n) for n in range(CH)] + [("wkT", n) for n in range(CH)] + [("wvT", n) for n in range(CH)]
                 + [("m", n) for n in range(CH)] + [("vo", n) for n in range(CH)]
                 + [("upT", 0), ("t1", 0), ("t2", 0)] + [("ff", n) for n in range(CH)]
                 + [("u_bias", 0), ("wqbk", 0), ("bvo", 0), ("scT", 0)]
                 + [("mod", n) for n in range(KINDS)] + [("cols", 0)])
        number = {key: n for n, key in enumerate(order)}
        split = [key for key in order if key[0] in ("m", "vo", "ff")]

        def bank(key):
            return banks[number[key] % NBANK]

        mod_half = KINDS // 2
        ROW_STEPS = 13

        with nc.Block() as block:
            @block.sync
            def _(sp):
                by_rows = lambda w: w.rearrange("(c p) n -> p c n", p=P)
                for w, t in ((g["Wq"], wq_sb), (g["Wk"], wk_sb)):
                    sp.dma_start(t[:], by_rows(w)).then_inc(in_qk, 16)
                for w, t in ((g["Wv"], wv_sb), (g["Wo"], wo_sb)):
                    sp.dma_start(t[:], by_rows(w)).then_inc(in_vo, 16)
                sp.dma_start(w_sb[:], by_rows(g["W"])).then_inc(in_w, 16)
                wm = by_rows(g["wmod"])
                sp.dma_start(wmod_sb[:], wm[:, :, 0:mod_half * D]).then_inc(in_mod0, 16)
                sp.wait_ge(made, number[("mod", mod_half - 1)] + 1)
                sp.dma_start(wmod_sb[:], wm[:, :, mod_half * D:]).then_inc(in_mod1, 16)
                for n, (rows, t) in enumerate(((g["ga_rows"], gate[:, 0, :]), (g["r1_rows"], r1[:]),
                                               (g["z_rows"], z[:]), (g["gb_rows"], gate[:, 1, :]),
                                               (g["r2_rows"], r2[:]))):
                    if n == 0:
                        sp.wait_ge(row_step, ROW_STEPS)
                    sp.dma_start(rows, t).then_inc(rows_out, 16)
                sp.wait_ge(rows_out, 16 * 5)

            @block.scalar
            def _(act):
                act.dma_start(c_sb[:], g["c"]).then_inc(in_c, 16)
                act.wait_ge(up_zero, 1)
                small = [(up_sb[:, :, 0:UDIM], g["up_aux"].rearrange("(c p) n -> p c n", p=P)),
                         (down_sb[:], g["down_aux"]),
                         (ldT[:], g["lora_down"].rearrange("r d -> d r")),
                         (luT[:], g["lora_up"].rearrange("u r -> r u"))]
                small += [(t[:], v.rearrange("(c p) -> p c", p=P))
                          for t, v in ((bq_col, g["bq"]), (bk_col, g["bk"]), (bv_col, g["bv"]))]
                small += [(t[:], v.partition_broadcast(B))
                          for t, v in ((bq_r, g["bq"]), (bk_r, g["bk"]), (bo_r, g["bo"]), (b_r, g["b"]))]
                assert len(small) == 11
                with nc.allow_non_contiguous_dma(reason="small"):
                    for t, v in small:
                        act.dma_start(t, v).then_inc(in_small, 16)
                act.wait_ge(in_c, 16)
                nc.scalar.activation(silu_e[:], c_sb[:], ACT.Exp, scale=-1.0).then_inc(e_made, 1)
                for n, key in enumerate(split):
                    act.wait_ge(made, number[key] + 1)
                    dst = {"m": m_w, "vo": vo_w, "ff": ff_w}[key[0]]
                    nc.scalar.activation(dst[:, HI, key[1], :], bank(key)[:], ACT.Copy).then_inc(hi_made, 1)

            @block.gpsimd
            def _(pool):
                nc.gpsimd.memset(up_sb[:], 0.0).then_inc(up_zero, 1)
                nc.gpsimd.memset(ident[:], 0.0).then_inc(id_zero, 1)
                pool.wait_ge(id_zero, 1)
                nc.gpsimd.affine_select(out=ident[:], in_=ident[:], compare_op=ALU.not_equal, fill=1.0, base=0,
                                        pattern=[[-1, P]], channel_multiplier=1).then_inc(id_made, 1)

            @block.tensor
            def _(pe):
                def product(key, *need):
                    n = number[key]
                    at = [number[k] + 1 for k in need] + ([n - NBANK + 1] if n >= NBANK else [])
                    if at:
                        pe.wait_ge(taken, max(at))
                    return bank(key)

                def transposes(key, src):
                    o = product(key)
                    for j in range(CH):
                        last = pe.transpose(o[:, j * P:(j + 1) * P], src[:, j, key[1] * P:(key[1] + 1) * P], ident[:])
                    last.then_inc(made, 1)

                def times(o, lhs, rhs):
                    for j in range(CH):
                        last = pe.matmul(o, lhs(j), rhs(j), start=(j == 0), stop=(j == CH - 1))
                    return last

                chunk = lambda n: slice(n * P, (n + 1) * P)
                pe.wait_ge(id_made, 1)
                pe.wait_ge(in_qk, 32)
                for n in range(CH):
                    transposes(("wqT", n), wq_sb)
                for n in range(CH):
                    transposes(("wkT", n), wk_sb)
                pe.wait_ge(in_vo, 32)
                for n in range(CH):
                    transposes(("wvT", n), wv_sb)
                for n in range(CH):
                    o = product(("m", n), ("wkT", CH - 1))
                    times(o[:], lambda j: wqT[:, j, chunk(n)], lambda j: wkT[:, j, :]).then_inc(made, 1)
                for n in range(CH):
                    o = product(("vo", n), ("wvT", CH - 1))
                    times(o[:], lambda j: wvT[:, j, chunk(n)], lambda j: wo_sb[:, j, :]).then_inc(made, 1)
                pe.wait_ge(in_small, 16 * 11)
                o = product(("upT", 0))
                for j in range(CH):
                    last = pe.transpose(o[:, chunk(j)], up_sb[:, j, :], ident[:])
                last.then_inc(made, 1)
                o = product(("t1", 0))
                pe.matmul(o[0:RANK, :], ldT[:], down_sb[:], start=True, stop=True).then_inc(made, 1)
                o = product(("t2", 0), ("t1", 0))
                pe.matmul(o[0:UDIM, :], luT[:], t1_sb[:], start=True, stop=True).then_inc(made, 1)
                pe.wait_ge(in_w, 16)
                for n in range(CH):
                    o = product(("ff", n), ("t2", 0), ("upT", 0))
                    for j in range(CH):
                        pe.matmul(o[:, chunk(j)], w_sb[:, j, chunk(n)], ident[:], start=(j == 0), stop=False)
                    pe.matmul(o[:], t2_sb[:, chunk(n)], upT[0:UDIM, :], start=False, stop=True).then_inc(made, 1)
                o = product(("u_bias", 0))
                for n in range(CH):
                    last = times(o[:, n:n + 1], lambda j: wkT[:, j, chunk(n)], lambda j: bq_col[:, j:j + 1])
                last.then_inc(made, 1)
                pe.wait_ge(reps, 2)
                o = product(("wqbk", 0))
                times(o[0:B, :], lambda j: bk_rep[:, j, :], lambda j: wqT[:, j, :]).then_inc(made, 1)
                o = product(("bvo", 0))
                times(o[0:B, :], lambda j: bv_rep[:, j, :], lambda j: wo_sb[:, j, :]).then_inc(made, 1)
                pe.wait_ge(silu_step, 3)
                o = product(("scT", 0))
                for j in range(CH):
                    last = pe.transpose(o[:, j * B:(j + 1) * B], silu_c[:, chunk(j)], ident[0:B, 0:B])
                last.then_inc(made, 1)
                for k in range(KINDS):
                    pe.wait_ge(in_mod0 if k < mod_half else in_mod1, 16)
                    at = (k % mod_half) * D
                    o = product(("mod", k), ("scT", 0))
                    times(o[0:B, :], lambda j: scT[:, j * B:(j + 1) * B],
                          lambda j: wmod_sb[:, j, at:at + D]).then_inc(made, 1)
                o = product(("cols", 0), ("mod", KINDS - 1))
                for q, kind in enumerate((CA, SA, CB, SB)):
                    for j in range(CH):
                        at = (q * CH + j) * B
                        last = pe.transpose(o[:, at:at + B], mod[:, kind, chunk(j)], ident[0:B, 0:B])
                last.then_inc(made, 1)

            @block.vector
            def _(dve):
                dve.wait_ge(e_made, 1)
                dve.tensor_scalar(silu_d[:], silu_e[:], 1.0, None, ALU.add).then_inc(silu_step, 1)
                dve.wait_ge(silu_step, 1)
                dve.reciprocal(silu_r[:], silu_d[:]).then_inc(silu_step, 1)
                dve.wait_ge(silu_step, 2)
                dve.tensor_tensor(silu_c[:], c_sb[:], silu_r[:], ALU.mult).then_inc(silu_step, 1)
                dve.wait_ge(in_small, 16 * 11)
                for rep, col in ((bk_rep, bk_col), (bv_rep, bv_col)):
                    dve.tensor_copy(rep[:], col[:].unsqueeze(2).to_broadcast([P, CH, B])).then_inc(reps, 1)
                for key in order:
                    kind, n = key
                    o = bank(key)
                    if key in split:
                        dve.wait_ge(hi_made, split.index(key) + 1)
                        dst = {"m": m_w, "vo": vo_w, "ff": ff_w}[kind]
                        dve.tensor_tensor(dst[:, LO, n, :], o[:], dst[:, HI, n, :].bitcast(F32),
                                          ALU.subtract).then_inc(taken, 1)
                        continue
                    dve.wait_ge(made, number[key] + 1)
                    if kind in ("wqT", "wkT", "wvT"):
                        last = dve.tensor_copy({"wqT": wqT, "wkT": wkT, "wvT": wvT}[kind][:, n, :], o[:])
                    elif kind == "upT":
                        last = dve.tensor_copy(upT[:], o[:])
                    elif kind == "t1":
                        last = dve.tensor_copy(t1_sb[:], o[0:RANK, :])
                    elif kind == "t2":
                        last = dve.tensor_copy(t2_sb[:], o[0:UDIM, :])
                    elif kind == "u_bias":
                        last = dve.tensor_copy(u_bias[:], o[:, 0:CH])
                    elif kind == "wqbk":
                        last = dve.tensor_copy(wqbk[:], o[0:B, :])
                    elif kind == "bvo":
                        last = dve.tensor_tensor(bvo[:], o[0:B, :], bo_r[:], ALU.add)
                    elif kind == "scT":
                        last = dve.tensor_copy(scT[:], o[:, 0:CH * B])
                    elif kind == "mod":
                        last = dve.tensor_scalar(mod[:, n, :], o[0:B, :], 1.0 if n in (CA, CB) else 0.0, None, ALU.add)
                    else:
                        last = dve.tensor_copy(cols[:].rearrange("p (b q) -> p b q", b=B),
                                               o[:, 0:4 * CH * B].rearrange("p (q b) -> p b q", b=B))
                    last.then_inc(taken, 1)
                dve.wait_ge(taken, len(order))
                step = [0]

                def row(ins, wait=True):
                    step[0] += 1
                    ins.then_inc(row_step, 1)
                    if wait:
                        dve.wait_ge(row_step, step[0])

                for n, kind in enumerate((GA, GB)):
                    row(dve.tensor_scalar(sign[:, n, :], mod[:, kind, :], 0.0, 2.0, ALU.is_ge, ALU.mult), False)
                    row(dve.scalar_tensor_tensor(size[:, n, :], mod[:, kind, :], -1.0, mod[:, kind, :], ALU.mult, ALU.max))
                    row(dve.tensor_scalar(magn[:, n, :], size[:, n, :], GATE_MIN, None, ALU.max))
                    row(dve.scalar_tensor_tensor(gate[:, n, :], sign[:, n, :], -1.0, magn[:, n, :], ALU.add, ALU.mult))
                row(dve.tensor_tensor(r1[:], gate[:, 0, :], bvo[:], ALU.mult), False)
                row(dve.tensor_tensor(r2[:], gate[:, 1, :], b_r[:], ALU.mult), False)
                row(dve.tensor_tensor(z[:, 0:D], mod[:, CA, :], wqbk[:], ALU.mult), False)
                row(dve.tensor_tensor_reduce(prod[:], bq_r[:], bk_r[:], 1.0, 0.0, ALU.mult, ALU.add, bqbk[:]))
                row(dve.tensor_tensor_reduce(prod[:], mod[:, SA, :], wqbk[:], 1.0, bqbk[:], ALU.mult, ALU.add,
                                             z[:, D:D + 1]))
                assert step[0] == ROW_STEPS


def run(nc, env, sem):
    g = env
    B, D, CH, TPB, N, SCALE, ZW = (g[k] for k in ("B", "D", "CH", "TPB", "N", "SCALE", "ZW"))
    hT, uT, v_sb, pT, h2T, x_sb = (g[k] for k in ("hT", "uT", "v_sb", "pT", "h2T", "x_sb"))
    n1, n2, h1, h2, exp_a, exp_b, prob_a, prob = (
        g[k] for k in ("n1", "n2", "h1", "h2", "exp_a", "exp_b", "prob_a", "prob"))
    gated_y, gated_o, junk = (g[k] for k in ("gated_y", "gated_o", "junk"))
    z_row, ga_row, gb_row, r1_row, r2_row, cols1, cols2 = (
        g[k] for k in ("z_row", "ga_row", "gb_row", "r1_row", "r2_row", "cols1", "cols2"))
    bank_u, bank_v, bank_s, bank_t1, bank_t2, bank_y, bank_o = (
        g[k] for k in ("bank_u", "bank_v", "bank_s", "bank_t1", "bank_t2", "bank_y", "bank_o"))
    ident, m_w, vo_w, ff_w, u_bias, cols = (g[k] for k in ("ident", "m_w", "vo_w", "ff_w", "u_bias", "cols"))
    kap, kap_s, sums, share = (g[k] for k in ("kap", "kap_s", "sums", "share"))
    scores = bank_s[:, 0:2 * P]
    probT = bank_s[:, 2 * P:4 * P]

    LOAD, LN1, T1, U, FF2, FF1 = 11, 8, 7, 3, -3, -2
    FIRST, LAST = -LOAD, N - 1 - FF2
    LOOP = XRING - LOAD
    ROUNDS = B - 1

    x_in = [sem(f"x_in{n}") for n in range(XRING)]
    x_out = [sem(f"x_out{n}") for n in range(XRING)]
    z_in, ga_in, gb_in, r1_in, r2_in = [sem(n) for n in ("z_in", "ga_in", "gb_in", "r1_in", "r2_in")]
    u_made, t1_made, s_made, v_made, pt_made, y_made, t2_made, o_made = [
        sem(f"{n}_made") for n in ("u", "t1", "s", "v", "pt", "y", "t2", "o")]
    cols1_set, cols2_set, u_hi, pt_hi, h1_made, h2_made, exp_made, v_hi = [
        sem(n) for n in ("cols1_set", "cols2_set", "u_hi", "pt_hi", "h1_made", "h2_made", "exp_made", "v_hi")]
    dve_init, u_lo, pt_lo, v_lo, h1_hi, h2_hi = [
        sem(n) for n in ("dve_init", "u_lo", "pt_lo", "v_lo", "h1_hi", "h2_hi")]
    st1_made, mv1_made, ve1_made, n1_made, kap_made, kap_scaled = [
        sem(n) for n in ("st1_made", "mv1_made", "ve1_made", "n1_made", "kap_made", "kap_scaled")]
    y_gated, x2_made, st2_made, mv2_made, ve2_made, n2_made, o_gated = [
        sem(n) for n in ("y_gated", "x2_made", "st2_made", "mv2_made", "ve2_made", "n2_made", "o_gated")]
    blk_made, win_made, maxk_made, neg_made, recip_made, weight_made, proba_made, prob_made = [
        sem(n) for n in ("blk_made", "win_made", "maxk_made", "neg_made", "recip_made", "weight_made",
                         "proba_made", "prob_made")]
    pool_init, h1_lo, h2_lo, rstd1_made, rstd2_made, r1_added, r2_added, out_made = [
        sem(n) for n in ("pool_init", "h1_lo", "h2_lo", "rstd1_made", "rstd2_made", "r1_added", "r2_added",
                         "out_made")]

    class Step:

        def __init__(self, s, i=None):
            self.s, self.i = s, i

        def has(self, t, end=N):
            return self.i is not None or 0 <= t < end

        def tile(self, t):
            return t if self.i is None else self.i + t

        def done(self, t):
            return self.tile(t + 1)

        def dma(self, t):
            return self.tile((t // TPB + 1) * TPB)

        def batch(self, t):
            return t // TPB if self.i is None else (self.i >> 4) + t // TPB

    assert TPB == 16

    def steps(engine, body):
        for s in range(FIRST, LOOP):
            body(Step(s))
        with engine.Fori(0, (ROUNDS - 1) * TPB + 1, TPB) as i:
            for s in range(LOOP, LOOP + TPB):
                body(Step(s, i))
        for s in range(LOOP + ROUNDS * TPB, LAST + 1):
            body(Step(s))

    def slot(t):
        at = HALF + t % RING * P
        return slice(at, at + P)

    def copies(t):
        if t % RING == 0:
            return [(slice(0, HALF), slice(HALF + RING * P, HALF + RING * P + HALF))]
        if t % RING == RING - 1:
            return [(slice(HALF, P), slice(0, HALF))]
        return []

    with nc.Block() as block:
        @block.sync
        def _(sp):
            def body(st):
                s = st.s
                def row(used, t, dst, rows, landed):
                    if t % TPB != TPB - 1 or not st.has(t + 1):
                        return
                    if t >= 0:
                        sp.wait_ge(used, st.done(t))
                    sp.dma_start(dst[:], rows[bass.ds(st.batch(t + 1), 1), :].rearrange("o d -> (o d)")
                                 .partition_broadcast(P)).then_inc(landed, 16)

                row(kap_made, s + LN1 - 1, z_row, g["z_rows"], z_in)
                row(r1_added, s + LN1 - 1, r1_row, g["r1_rows"], r1_in)
                row(y_gated, s - 2, ga_row, g["ga_rows"], ga_in)
                row(r2_added, s - 2, r2_row, g["r2_rows"], r2_in)
                row(o_gated, s + FF2 - 1, gb_row, g["gb_rows"], gb_in)
                t = s + FF2
                if st.has(t):
                    sp.wait_ge(out_made, st.done(t))
                    sp.dma_start(g["out_t"][st.tile(t)], x_sb[:, t % XRING, :]).then_inc(x_out[t % XRING], 16)
                t = s + LOAD
                if st.has(t):
                    if st.has(t - XRING):
                        sp.wait_ge(x_out[t % XRING], st.dma(t - XRING))
                    sp.dma_start(x_sb[:, t % XRING, :], g["x_t"][st.tile(t)]).then_inc(x_in[t % XRING], 16)

            steps(sp, body)
            for n in range(XRING):
                sp.wait_ge(x_out[n], 16 * B)

        @block.tensor
        def _(pe):
            def three(o, left, right, start=True, stop=True):
                pe.matmul(o, left(HI), right(HI), start=start, stop=False)
                pe.matmul(o, left(HI), right(LO), start=False, stop=False)
                return pe.matmul(o, left(LO), right(HI), start=False, stop=stop)

            def body(st):
                s = st.s
                t = s + U
                if st.has(t):
                    grp, ch = t // GROUP, t % GROUP
                    pe.wait_ge(h1_lo, st.done(grp * GROUP + GROUP - 1))
                    if st.has(t - 1):
                        pe.wait_ge(u_lo, st.done(t - 1))
                    at = HALF + grp % 2 * GROUP * P
                    for k in range(CH):
                        last = three(bank_u[:], lambda w: m_w[:, w, k, ch * P:(ch + 1) * P],
                                     lambda w: hT[:, w, k, at:at + GROUP * P], k == 0, k == CH - 1)
                    last.then_inc(u_made, 1)
                t = s - 1
                if st.has(t):
                    pe.wait_ge(prob_made, st.done(t))
                    for k in range(2):
                        last = pe.transpose(probT[:, k * P:(k + 1) * P], prob[:, k * P:(k + 1) * P], ident[:])
                    last.then_inc(pt_made, 1)
                t = s + FF1
                if st.has(t):
                    pe.wait_ge(n2_made, st.done(t))
                    if st.has(t - 1):
                        pe.wait_ge(h2_made, st.done(t - 1))
                    for k in range(CH):
                        last = pe.transpose(bank_t2[:, k * P:(k + 1) * P], n2[:, k * P:(k + 1) * P], ident[:])
                    last.then_inc(t2_made, 1)
                t = s + FF2
                if st.has(t):
                    pe.wait_ge(h2_lo, st.done(t))
                    if st.has(t - 1):
                        pe.wait_ge(o_gated, st.done(t - 1))
                    for k in range(CH):
                        last = three(bank_o[:], lambda w: h2T[:, t % 2, w, k, :], lambda w: ff_w[:, w, k, :],
                                     k == 0, k == CH - 1)
                    last.then_inc(o_made, 1)
                t = s - 1
                if st.has(t):
                    pe.wait_ge(pt_lo, st.done(t))
                    pe.wait_ge(v_lo, st.done(t + 1))
                    if st.has(t - 1):
                        pe.wait_ge(y_gated, st.done(t - 1))
                    for k in range(2):
                        last = three(bank_y[:], lambda w: pT[:, w, k * P:(k + 1) * P],
                                     lambda w: v_sb[:, (t + k) % 2, w, :], k == 0, k == 1)
                    last.then_inc(y_made, 1)
                t = s + T1
                if st.has(t):
                    pe.wait_ge(n1_made, st.done(t))
                    if st.has(t - 1):
                        pe.wait_ge(h1_made, st.done(t - 1))
                    for k in range(CH):
                        last = pe.transpose(bank_t1[:, k * P:(k + 1) * P], n1[:, k * P:(k + 1) * P], ident[:])
                    last.then_inc(t1_made, 1)
                t = s
                if st.has(t):
                    grp = t // GROUP
                    pe.wait_ge(u_lo, st.done(grp * GROUP + GROUP - 1))
                    if t == 0 and st.i is None:
                        pe.wait_ge(pool_init, 2)
                    at = t % RING * P
                    q = t % GROUP * P
                    for k in range(CH):
                        last = three(scores, lambda w: uT[:, grp % 2, w, k, q:q + P],
                                     lambda w: hT[:, w, k, at:at + 2 * P], k == 0, k == CH - 1)
                    last.then_inc(s_made, 1)
                t = s + 1
                if st.has(t, N + 1):
                    if t == 0 and st.i is None:
                        pe.wait_ge(pool_init, 2)
                    if st.has(t):
                        pe.wait_ge(h1_lo, st.done(t))
                    if st.has(t - 1):
                        pe.wait_ge(v_lo, st.done(t - 1))
                    at = t % RING * P
                    for k in range(CH):
                        last = three(bank_v[:], lambda w: hT[:, w, k, at:at + P], lambda w: vo_w[:, w, k, :],
                                     k == 0, k == CH - 1)
                    last.then_inc(v_made, 1)

            steps(pe, body)

        @block.scalar
        def _(act):
            def modulate(st, t, dst, src, cur, first, set_sem, made, ready, free, free_t):
                if t % TPB == 0:
                    at = st.batch(t) * (4 * CH) + first
                    act.copy(cur[:], cols[:, bass.ds(at, 2 * CH)]).then_inc(set_sem, 1)
                    act.wait_ge(set_sem, st.batch(t) + 1)
                act.wait_ge(ready, st.done(t))
                if st.has(free_t):
                    act.wait_ge(free, st.done(free_t))
                for k in range(CH):
                    last = act.activation(dst[:, k, :], src[:, k * P:(k + 1) * P], ACT.Identity,
                                          bias=cur[:, CH + k:CH + k + 1], scale=cur[:, k:k + 1])
                last.then_inc(made, 1)

            def body(st):
                s = st.s
                t = s + U
                if st.has(t):
                    grp, ch = t // GROUP, t % GROUP
                    act.wait_ge(u_made, st.done(t))
                    act.activation(uT[:, grp % 2, HI, ch, :], bank_u[:], ACT.Identity,
                                   bias=u_bias[:, ch:ch + 1]).then_inc(u_hi, 1)
                t = s - 1
                if st.has(t):
                    act.wait_ge(pt_made, st.done(t))
                    act.activation(pT[:, HI, :], probT, ACT.Copy).then_inc(pt_hi, 1)
                t = s + FF1
                if st.has(t):
                    modulate(st, t, h2, bank_t2, cols2, 2 * CH, cols2_set, h2_made, t2_made, h2_lo, t - 1)
                t = s + T1
                if st.has(t):
                    modulate(st, t, h1, bank_t1, cols1, 0, cols1_set, h1_made, t1_made, h1_lo, t - 1)
                t = s
                if st.has(t):
                    act.wait_ge(neg_made, st.done(t))
                    for half in range(2):
                        rows = slice(half * HALF, (half + 1) * HALF)
                        for w, dst in enumerate((exp_a, exp_b)):
                            keys = slice((half + w) * HALF, (half + w) * HALF + P)
                            last = act.activation(dst[rows, keys], scores[rows, keys], ACT.Exp,
                                                  bias=g["neg_max"][rows, half + w:half + w + 1], scale=SCALE,
                                                  accum_out=sums[rows, w:w + 1])
                    last.then_inc(exp_made, 1)
                t = s + 1
                if st.has(t, N + 1):
                    act.wait_ge(v_made, st.done(t))
                    act.activation(v_sb[:, t % 2, HI, :], bank_v[:], ACT.Copy).then_inc(v_hi, 1)

            steps(act, body)

        @block.vector
        def _(dve):
            def low(dst, src, high, made):
                dve.tensor_tensor(dst, src, high.bitcast(F32), ALU.subtract).then_inc(made, 1)

            def variance(st, t, src, stats, mv, ve, st_made, mv_made, ve_made):
                dve.bn_stats(stats[:], src).then_inc(st_made, 1)
                dve.wait_ge(st_made, st.done(t))
                dve.memset(g["spare"][:], 0.0)
                dve.bn_aggr(mv[:], stats[:]).then_inc(mv_made, 1)
                dve.wait_ge(mv_made, st.done(t))
                dve.tensor_scalar(ve[:], mv[:, 1:2], LN_EPS, None, ALU.add).then_inc(ve_made, 1)

            def normalise(dst, src, mv, rstd, made):
                dve.tensor_scalar(dst[:], src, mv[:, 0:1], rstd[:], ALU.subtract, ALU.mult).then_inc(made, 1)

            dve.memset(exp_a[:], 0.0)
            dve.memset(exp_b[:], 0.0)
            dve.memset(share[:], 0.5).then_inc(dve_init, 1)
            dve.wait_ge(dve_init, 1)
            dve.memset(share[0:HALF, 0, 0:1], 0.0)
            dve.memset(share[0:HALF, 0, 1:2], 1.0)
            dve.memset(share[HALF:P, 2, 0:1], 1.0)
            dve.memset(share[HALF:P, 2, 1:2], 0.0).then_inc(dve_init, 1)
            dve.wait_ge(dve_init, 2)

            def body(st):
                s = st.s
                t = s + U
                if st.has(t):
                    grp, ch = t // GROUP, t % GROUP
                    dve.wait_ge(u_hi, st.done(t))
                    dve.scalar_tensor_tensor(uT[:, grp % 2, LO, ch, :], bank_u[:], u_bias[:, ch:ch + 1],
                                             uT[:, grp % 2, HI, ch, :].bitcast(F32), ALU.add,
                                             ALU.subtract).then_inc(u_lo, 1)
                t = s - 1
                if st.has(t):
                    dve.wait_ge(pt_hi, st.done(t))
                    low(pT[:, LO, :], probT, pT[:, HI, :], pt_lo)
                t = s + FF1
                if st.has(t):
                    dve.wait_ge(h2_made, st.done(t))
                    dve.tensor_copy(h2T[:, t % 2, HI, :, :], h2[:]).then_inc(h2_hi, 1)
                t = s + FF2
                if st.has(t):
                    dve.wait_ge(o_made, st.done(t))
                    if t % TPB == 0:
                        dve.wait_ge(gb_in, st.dma(t))
                    if st.has(t - 1):
                        dve.wait_ge(out_made, st.done(t - 1))
                    dve.tensor_tensor(gated_o[:], bank_o[:], gb_row[:], ALU.mult).then_inc(o_gated, 1)
                t = s - 1
                if st.has(t):
                    dve.wait_ge(y_made, st.done(t))
                    if t % TPB == 0:
                        dve.wait_ge(ga_in, st.dma(t))
                    dve.tensor_tensor(gated_y[:], bank_y[:], ga_row[:], ALU.mult).then_inc(y_gated, 1)
                    dve.wait_ge(y_gated, st.done(t))
                    dve.wait_ge(r1_added, st.done(t))
                    xt = x_sb[:, t % XRING, :]
                    dve.tensor_tensor(xt, xt, gated_y[:], ALU.add).then_inc(x2_made, 1)
                    dve.wait_ge(x2_made, st.done(t))
                    variance(st, t, xt, g["stats2"], g["mv2"], g["ve2"], st2_made, mv2_made, ve2_made)
                t = s
                if st.has(t):
                    c = t % XRING
                    dve.wait_ge(s_made, st.done(t))
                    dve.reduce_max(g["blk_max"][:], scores.rearrange("p (b k) -> p b k", k=HALF),
                                   AX_X).then_inc(blk_made, 1)
                    dve.wait_ge(blk_made, st.done(t))
                    dve.tensor_tensor(g["win_max"][:], g["blk_max"][:, 0:3], g["blk_max"][:, 1:4],
                                      ALU.max).then_inc(win_made, 1)
                    dve.wait_ge(win_made, st.done(t))
                    dve.tensor_scalar(g["max_k"][:], g["win_max"][:], kap[:, c:c + 1], None,
                                      ALU.add).then_inc(maxk_made, 1)
                    dve.wait_ge(maxk_made, st.done(t))
                    dve.tensor_scalar(g["neg_max"][:], g["max_k"][:], -SCALE, kap_s[:, c:c + 1], ALU.mult,
                                      ALU.add).then_inc(neg_made, 1)
                t = s + T1
                if st.has(t):
                    dve.wait_ge(h1_made, st.done(t))
                    if st.has(s):
                        dve.wait_ge(s_made, st.done(s))
                    for src, dst in copies(t):
                        dve.tensor_copy(hT[:, HI, :, dst], h1[:, :, src])
                    dve.tensor_copy(hT[:, HI, :, slot(t)], h1[:]).then_inc(h1_hi, 1)
                t = s - 1
                if st.has(t):
                    dve.wait_ge(rstd2_made, st.done(t))
                    if st.has(t - 1):
                        dve.wait_ge(t2_made, st.done(t - 1))
                    normalise(n2, x_sb[:, t % XRING, :], g["mv2"], g["rstd2"], n2_made)
                t = s + LN1
                if st.has(t):
                    dve.wait_ge(x_in[t % XRING], st.dma(t))
                    variance(st, t, x_sb[:, t % XRING, :], g["stats1"], g["mv1"], g["ve1"], st1_made, mv1_made,
                             ve1_made)
                t = s
                if st.has(t):
                    edge = {0: 0, TPB - 1: 2}.get(t % TPB, 1)
                    dve.wait_ge(exp_made, st.done(t))
                    dve.reciprocal(g["recips"][:], sums[:]).then_inc(recip_made, 1)
                    dve.wait_ge(recip_made, st.done(t))
                    dve.tensor_tensor(g["weights"][:], g["recips"][:], share[:, edge, :],
                                      ALU.mult).then_inc(weight_made, 1)
                    dve.wait_ge(weight_made, st.done(t))
                    dve.tensor_scalar(prob_a[:], exp_a[:], g["weights"][:, 0:1], None,
                                      ALU.mult).then_inc(proba_made, 1)
                    dve.wait_ge(proba_made, st.done(t))
                    dve.scalar_tensor_tensor(prob[:], exp_b[:], g["weights"][:, 1:2], prob_a[:], ALU.mult,
                                             ALU.add).then_inc(prob_made, 1)
                t = s + 1
                if st.has(t, N + 1):
                    dve.wait_ge(v_hi, st.done(t))
                    low(v_sb[:, t % 2, LO, :], bank_v[:], v_sb[:, t % 2, HI, :], v_lo)
                t = s + LN1
                if st.has(t):
                    c = t % XRING
                    dve.wait_ge(rstd1_made, st.done(t))
                    if st.has(t - 1):
                        dve.wait_ge(t1_made, st.done(t - 1))
                    normalise(n1, x_sb[:, c, :], g["mv1"], g["rstd1"], n1_made)
                    dve.wait_ge(n1_made, st.done(t))
                    if t % TPB == 0:
                        dve.wait_ge(z_in, st.dma(t))
                    dve.tensor_tensor_reduce(junk[:], n1[:], z_row[:, 0:D], 1.0, z_row[:, D:D + 1], ALU.mult,
                                             ALU.add, kap[:, c:c + 1]).then_inc(kap_made, 1)
                    dve.wait_ge(kap_made, st.done(t))
                    dve.tensor_scalar(kap_s[:, c:c + 1], kap[:, c:c + 1], SCALE, None,
                                      ALU.mult).then_inc(kap_scaled, 1)

            steps(dve, body)

        @block.gpsimd
        def _(pool):
            def low(dst, src, high):
                return pool.tensor_tensor(dst, src, high.bitcast(F32), ALU.subtract)

            def add_row(t, row, made):
                xt = x_sb[:, t % XRING, :]
                pool.tensor_tensor(xt, xt, row, ALU.add).then_inc(made, 1)

            pool.memset(g["minus_half"][:], -0.5).then_inc(pool_init, 1)
            pool.memset(hT[:, :, :, 0:HALF].bitcast(F32), 0.0).then_inc(pool_init, 1)
            pool.wait_ge(pool_init, 2)

            def body(st):
                s = st.s
                t = s + FF1
                if st.has(t):
                    pool.wait_ge(h2_hi, st.done(t))
                    low(h2T[:, t % 2, LO, :, :], h2[:], h2T[:, t % 2, HI, :, :]).then_inc(h2_lo, 1)
                t = s + FF2
                if st.has(t):
                    pool.wait_ge(o_gated, st.done(t))
                    pool.wait_ge(r2_added, st.done(t))
                    add_row(t, gated_o[:], out_made)
                t = s - 1
                if st.has(t):
                    pool.wait_ge(ve2_made, st.done(t))
                    pool.tensor_tensor(g["rstd2"][:], g["ve2"][:], g["minus_half"][:], ALU.pow).then_inc(rstd2_made, 1)
                t = s + T1
                if st.has(t):
                    pool.wait_ge(h1_hi, st.done(t))
                    for src, dst in copies(t):
                        low(hT[:, LO, :, dst], h1[:, :, src], hT[:, HI, :, dst])
                    low(hT[:, LO, :, slot(t)], h1[:], hT[:, HI, :, slot(t)]).then_inc(h1_lo, 1)
                t = s + LN1
                if st.has(t):
                    pool.wait_ge(ve1_made, st.done(t))
                    pool.tensor_tensor(g["rstd1"][:], g["ve1"][:], g["minus_half"][:], ALU.pow).then_inc(rstd1_made, 1)
                t = s - 1
                if st.has(t):
                    pool.wait_ge(n2_made, st.done(t))
                    if t % TPB == 0:
                        pool.wait_ge(r2_in, st.dma(t))
                    add_row(t, r2_row[:], r2_added)
                t = s + LN1
                if st.has(t):
                    pool.wait_ge(n1_made, st.done(t))
                    if t % TPB == 0:
                        pool.wait_ge(r1_in, st.dma(t))
                    add_row(t, r1_row[:], r1_added)

            steps(pool, body)


_INS = ['L0_attn_x', 'L0_attn_Wq', 'L0_attn_bq', 'L0_attn_Wk', 'L0_attn_bk', 'L0_attn_Wv', 'L0_attn_bv', 'L0_attn_Wo',
        'L0_attn_bo', 'L0_ffn_W', 'L0_ffn_b', 'L0_ffn_lora_down', 'L0_ffn_lora_up', 'L0_ffn_down_aux',
        'L0_ffn_up_aux', 'L0_c', 'L0_wmod']


def kernel(**inputs):
    import numpy as _np
    import concourse.bacc as _bacc
    from concourse import mybir as _mybir
    from concourse.bass_utils import run_bass_kernel_spmd as _run

    nc = _bacc.Bacc("TRN2", target_bir_lowering=False, num_devices=1)
    arrays, args = {}, []
    for name in _INS:
        a = _np.ascontiguousarray(inputs[name])
        arrays[f"in_{name}_dram"] = a
        args.append(nc.dram_tensor(f"in_{name}_dram", a.shape, _mybir.dt.from_np(a.dtype), kind="ExternalInput").ap())
    shape = inputs['L0_attn_x'].shape
    args.append(nc.dram_tensor("out_0_dram", shape, _mybir.dt.float32, kind="ExternalOutput").ap())
    adaln_block_kernel(nc, *args)
    r = _run(nc, [arrays], core_ids=[0])
    return r.results[0]["out_0_dram"]
```

```python
from contextlib import ExitStack

import concourse.bass as bass
from concourse import mybir

ALU = mybir.AluOpType
ACT = mybir.ActivationFunctionType
AX_X = mybir.AxisListType.X
F32 = mybir.dt.float32
F32R = mybir.dt.float32r
HI, LO = 0, 1

P = 128
HALF = P // 2
HEAD_DIM = 32
LN_EPS = 1e-5
GATE_MIN = 0.25

RING = 8
GROUP = 4
XRING = 16


def adaln_block_kernel(nc, x, Wq, bq, Wk, bk, Wv, bv, Wo, bo, W, b, lora_down, lora_up, down_aux, up_aux,
                       c, wmod, out):
    B, S, D = x.shape
    CH = D // P
    TPB = S // P
    N = B * TPB
    RANK, DDIM = lora_down.shape
    UDIM = lora_up.shape[0]
    KINDS = wmod.shape[1] // D
    SA, CA, GA, SB, CB, GB = range(KINDS)
    SCALE = float(HEAD_DIM) ** -0.5
    ZW = D + 1
    assert TPB == XRING and TPB % RING == 0 and RING == 2 * GROUP and CH * P == D

    x_t = x.rearrange("b (t p) d -> (b t) p d", p=P)
    out_t = out.rearrange("b (t p) d -> (b t) p d", p=P)

    with ExitStack() as ctx:
        def sb(name, shape, dt=F32, stack=ctx):
            return stack.enter_context(nc.sbuf_tensor(name, shape, dt))

        def sem(name):
            return ctx.enter_context(nc.semaphore(name))

        bank_u, bank_v, bank_s, bank_t1, bank_t2, bank_y, bank_o, bank_x = [
            ctx.enter_context(nc.psum_tensor(f"bank_{n}", [P, 512], F32))
            for n in ("u", "v", "s", "t1", "t2", "y", "o", "x")]

        ident = sb("ident", [P, P])
        m_w = sb("m_w", [P, 2, CH, D], F32R)
        vo_w = sb("vo_w", [P, 2, CH, D], F32R)
        ff_w = sb("ff_w", [P, 2, CH, D], F32R)
        u_bias = sb("u_bias", [P, CH])
        cols = sb("cols", [P, B * 4 * CH])
        z_rows = nc.dram_tensor("z_rows", [B, ZW], F32, kind="Internal").ap()
        ga_rows = nc.dram_tensor("ga_rows", [B, D], F32, kind="Internal").ap()
        gb_rows = nc.dram_tensor("gb_rows", [B, D], F32, kind="Internal").ap()
        r1_rows = nc.dram_tensor("r1_rows", [B, D], F32, kind="Internal").ap()
        r2_rows = nc.dram_tensor("r2_rows", [B, D], F32, kind="Internal").ap()

        carried = ExitStack()
        wvT = sb("wvT", [P, CH, D], F32, carried)
        wo_sb = sb("wo_sb", [P, CH, D], F32, carried)
        w_sb = sb("w_sb", [P, CH, D], F32, carried)
        t2_sb = sb("t2_sb", [UDIM, D], F32, carried)
        upT = sb("upT", [P, D], F32, carried)
        in_o, in_w, rows_out = sem("in_o"), sem("in_w"), sem("rows_out")

        prepare(nc, locals(), sem)
        carried.close()

        main = ExitStack()
        with main:
            ms = lambda name, shape, dt=F32: sb(name, shape, dt, main)
            uT = ms("uT", [P, 2, 2, CH, GROUP * P], F32R)
            hT = ms("hT", [P, 2, CH, HALF + RING * P + HALF], F32R)
            v_sb = ms("v_sb", [P, 2, 2, D], F32R)
            pT = ms("pT", [P, 2, 2 * P], F32R)
            h2T = ms("h2T", [P, 2, 2, CH, P], F32R)
            x_sb = ms("x_sb", [P, XRING, D])
            n1 = ms("n1", [P, D])
            n2 = ms("n2", [P, D])
            h1 = ms("h1", [P, CH, P])
            h2 = ms("h2", [P, CH, P])
            exp_a = ms("exp_a", [P, 2 * P])
            exp_b = ms("exp_b", [P, 2 * P])
            prob_a = ms("prob_a", [P, 2 * P])
            prob = ms("prob", [P, 2 * P])
            gated_y = ms("gated_y", [P, D])
            gated_o = ms("gated_o", [P, D])
            junk = ms("junk", [P, D])
            z_row = ms("z_row", [P, ZW])
            ga_row = ms("ga_row", [P, D])
            gb_row = ms("gb_row", [P, D])
            r1_row = ms("r1_row", [P, D])
            r2_row = ms("r2_row", [P, D])
            cols1 = ms("cols1", [P, 2 * CH])
            cols2 = ms("cols2", [P, 2 * CH])
            stats1 = ms("stats1", [P, 6])
            stats2 = ms("stats2", [P, 6])
            mv1 = ms("mv1", [P, 2])
            mv2 = ms("mv2", [P, 2])
            ve1 = ms("ve1", [P, 1])
            ve2 = ms("ve2", [P, 1])
            rstd1 = ms("rstd1", [P, 1])
            rstd2 = ms("rstd2", [P, 1])
            minus_half = ms("minus_half", [P, 1])
            spare = ms("spare", [P, 1])
            kap = ms("kap", [P, XRING])
            kap_s = ms("kap_s", [P, XRING])
            blk_max = ms("blk_max", [P, 4])
            win_max = ms("win_max", [P, 3])
            max_k = ms("max_k", [P, 3])
            neg_max = ms("neg_max", [P, 3])
            sums = ms("sums", [P, 2])
            recips = ms("recips", [P, 2])
            weights = ms("weights", [P, 2])
            share = ms("share", [P, 3, 2])
            run(nc, locals(), sem)


def prepare(nc, env, sem):
    g = env
    B, D, CH, KINDS, ZW, RANK, DDIM, UDIM = (g[k] for k in ("B", "D", "CH", "KINDS", "ZW", "RANK", "DDIM", "UDIM"))
    SA, CA, GA, SB, CB, GB = range(KINDS)
    ident, m_w, u_bias, cols = (g[k] for k in ("ident", "m_w", "u_bias", "cols"))
    wvT, wo_sb, w_sb, t2_sb, upT = (g[k] for k in ("wvT", "wo_sb", "w_sb", "t2_sb", "upT"))
    in_o, in_w, rows_out = (g[k] for k in ("in_o", "in_w", "rows_out"))
    banks = [g[k] for k in ("bank_u", "bank_v", "bank_s", "bank_t1", "bank_t2", "bank_y", "bank_o", "bank_x")]
    NBANK = len(banks)

    with ExitStack() as ctx:
        def sb(name, shape, dt=F32):
            return ctx.enter_context(nc.sbuf_tensor(name, shape, dt))

        qk_sb = sb("qk_sb", [P, 2, CH, D])
        wq_sb, wk_sb = qk_sb[:, 0], qk_sb[:, 1]
        wv_sb = sb("wv_sb", [P, CH, D])
        wqT, wkT = [sb(f"{n}T", [P, CH, D]) for n in ("wq", "wk")]
        wmod_sb = [sb("wmod0_sb", [P, CH, 2 * D])[:], sb("wmod1_sb", [P, CH, 2 * D])[:],
                   qk_sb[:].rearrange("p a c d -> p (a c d)").rearrange("p (c n) -> p c n", c=CH)]
        c_sb = sb("c_sb", [B, D])
        silu_d = sb("silu_d", [B, D])
        silu_c = sb("silu_c", [B, D])
        scT = sb("scT", [P, CH * B])
        up_sb = sb("up_sb", [P, CH, P])
        down_sb = sb("down_sb", [DDIM, D])
        ldT = sb("ldT", [DDIM, RANK])
        luT = sb("luT", [RANK, UDIM])
        t1_sb = sb("t1_sb", [RANK, D])
        bq_r, bk_r, bv_r, bo_r, b_r = [sb(f"{n}_r", [B, D]) for n in ("bq", "bk", "bv", "bo", "bff")]
        rep = sb("rep", [P, 3 * CH * B])
        wqbk = sb("wqbk", [B, D])
        bvo = sb("bvo", [B, D])
        mod = sb("mod", [B, KINDS, D])
        gate = sb("gate", [B, 2, D])
        sign = sb("sign", [B, 2, D])
        size = sb("size", [B, 2, D])
        z = sb("z", [B, ZW])
        prod = sb("prod", [B, D])
        bqbk = sb("bqbk", [B, 1])
        r1 = sb("r1", [B, D])
        r2 = sb("r2", [B, D])

        in_q, in_k, in_v, in_c, in_rows, in_lora, in_mod0, in_mod1, in_mod2 = [
            sem(f"in_{n}") for n in ("q", "k", "v", "c", "rows", "lora", "mod0", "mod1", "mod2")]
        in_mod = [in_mod0, in_mod1, in_mod2]
        up_zero, id_zero, id_made = sem("up_zero"), sem("id_zero"), sem("id_made")
        e_made, silu_step, made = sem("e_made"), sem("silu_step"), sem("made")
        hi_made, taken_v, taken_s, row_step = sem("hi_made"), sem("taken_v"), sem("taken_s"), sem("row_step")

        order = ([("wqT", n) for n in range(CH)] + [("wkT", n) for n in range(CH)]
                 + [("m", n) for n in range(CH)] + [("wvT", n) for n in range(CH)]
                 + [("upT", 0), ("t1", 0), ("t2", 0), ("scT", 0)] + [("mod", n) for n in range(GA + 2)]
                 + [("rep", 0), ("wqbk", 0), ("bvo", 0)] + [("mod", n) for n in range(GA + 2, KINDS)]
                 + [("cols", 0), ("u_bias", 0)])
        number = {key: n for n, key in enumerate(order)}
        split = [key for key in order if key[0] == "m"]
        by_scalar = [key for key in order if key[0] in ("wqT", "wkT", "wvT") and key[1] % 2]
        by_vector = [key for key in order if key not in by_scalar]

        def taken(key):
            if key in by_scalar:
                return taken_s, by_scalar.index(key) + 1
            return taken_v, by_vector.index(key) + 1

        def bank(key):
            return banks[number[key] % NBANK]

        EARLY_ROWS, ALL_ROWS = 8, 13
        SMALL_ROWS = ((bq_r, g["bq"]), (bk_r, g["bk"]), (bv_r, g["bv"]), (bo_r, g["bo"]), (b_r, g["b"]))

        with nc.Block() as block:
            @block.sync
            def _(sp):
                by_rows = lambda w: w.rearrange("(c p) n -> p c n", p=P)
                wm = by_rows(g["wmod"])
                sp.dma_start(wq_sb, by_rows(g["Wq"])).then_inc(in_q, 16)
                sp.dma_start(wk_sb, by_rows(g["Wk"])).then_inc(in_k, 16)
                sp.dma_start(wv_sb[:], by_rows(g["Wv"])).then_inc(in_v, 16)
                sp.dma_start(wo_sb[:], by_rows(g["Wo"])).then_inc(in_o, 16)
                for n in range(3):
                    if n == 2:
                        sp.dma_start(w_sb[:], by_rows(g["W"])).then_inc(in_w, 16)
                        sp.wait_ge(made, number[("wkT", CH - 1)] + 1)
                    sp.dma_start(wmod_sb[n], wm[:, :, 2 * n * D:2 * (n + 1) * D]).then_inc(in_mod[n], 16)
                sp.wait_ge(row_step, EARLY_ROWS)
                for rows, t in ((g["ga_rows"], gate[:, 0, :]), (g["r1_rows"], r1[:]), (g["z_rows"], z[:])):
                    sp.dma_start(rows, t).then_inc(rows_out, 16)
                sp.wait_ge(row_step, ALL_ROWS)
                for rows, t in ((g["gb_rows"], gate[:, 1, :]), (g["r2_rows"], r2[:])):
                    sp.dma_start(rows, t).then_inc(rows_out, 16)
                sp.wait_ge(rows_out, 16 * 5)

            @block.scalar
            def _(act):
                act.dma_start(c_sb[:], g["c"]).then_inc(in_c, 16)
                for t, v in SMALL_ROWS:
                    act.dma_start(t[:], v.partition_broadcast(B)).then_inc(in_rows, 16)
                act.wait_ge(in_c, 16)
                nc.scalar.activation(silu_d[:], c_sb[:], ACT.Exp, scale=-1.0).then_inc(e_made, 1)
                act.wait_ge(up_zero, 1)
                with nc.allow_non_contiguous_dma(reason="small"):
                    for t, v in ((up_sb[:, :, 0:UDIM], g["up_aux"].rearrange("(c p) n -> p c n", p=P)),
                                 (down_sb[:], g["down_aux"]),
                                 (ldT[:], g["lora_down"].rearrange("r d -> d r")),
                                 (luT[:], g["lora_up"].rearrange("u r -> r u"))):
                        act.dma_start(t, v).then_inc(in_lora, 16)
                for key in order:
                    kind, n = key
                    if key in split:
                        act.wait_ge(made, number[key] + 1)
                        nc.scalar.activation(m_w[:, HI, n, :], bank(key)[:], ACT.Copy).then_inc(hi_made, 1)
                    elif key in by_scalar:
                        act.wait_ge(made, number[key] + 1)
                        dst = {"wqT": wqT, "wkT": wkT, "wvT": wvT}[kind]
                        nc.scalar.activation(dst[:, n, :], bank(key)[:], ACT.Copy).then_inc(taken_s, 1)

            @block.gpsimd
            def _(pool):
                nc.gpsimd.memset(ident[:], 0.0).then_inc(id_zero, 1)
                pool.wait_ge(id_zero, 1)
                nc.gpsimd.affine_select(out=ident[:], in_=ident[:], compare_op=ALU.not_equal, fill=1.0, base=0,
                                        pattern=[[-1, P]], channel_multiplier=1).then_inc(id_made, 1)
                nc.gpsimd.memset(up_sb[:], 0.0).then_inc(up_zero, 1)

            @block.tensor
            def _(pe):
                def product(key, *need):
                    n = number[key]
                    need = list(need) + ([order[n - NBANK]] if n >= NBANK else [])
                    for which in (taken_v, taken_s):
                        at = [v for w, v in map(taken, need) if w is which]
                        if at:
                            pe.wait_ge(which, max(at))
                    return bank(key)

                chunk = lambda n: slice(n * P, (n + 1) * P)

                def transposes(key, src):
                    o = product(key)
                    for j in range(CH):
                        last = pe.transpose(o[:, chunk(j)], src[:, j, chunk(key[1])], ident[:])
                    last.then_inc(made, 1)

                def times(o, lhs, rhs):
                    for j in range(CH):
                        last = pe.matmul(o, lhs(j), rhs(j), start=(j == 0), stop=(j == CH - 1))
                    return last

                def columns(o, at, row):
                    for j in range(CH):
                        last = pe.transpose(o[:, at + j * B:at + (j + 1) * B], row[:, chunk(j)], ident[0:B, 0:B])
                    return last

                both = lambda name: [(name, n) for n in range(CH)]
                rep_of = lambda n, j: rep[:, (n * CH + j) * B:(n * CH + j + 1) * B]
                pe.wait_ge(id_made, 1)
                pe.wait_ge(in_q, 16)
                for n in range(CH):
                    transposes(("wqT", n), wq_sb)
                pe.wait_ge(in_k, 16)
                for n in range(CH):
                    transposes(("wkT", n), wk_sb)
                for n in range(CH):
                    o = product(("m", n), *both("wqT"), *both("wkT"))
                    times(o[:], lambda j: wqT[:, j, chunk(n)], lambda j: wkT[:, j, :]).then_inc(made, 1)
                pe.wait_ge(in_v, 16)
                for n in range(CH):
                    transposes(("wvT", n), wv_sb)
                pe.wait_ge(in_lora, 16 * 4)
                o = product(("upT", 0))
                for j in range(CH):
                    last = pe.transpose(o[:, chunk(j)], up_sb[:, j, :], ident[:])
                last.then_inc(made, 1)
                o = product(("t1", 0))
                pe.matmul(o[0:RANK, :], ldT[:], down_sb[:], start=True, stop=True).then_inc(made, 1)
                o = product(("t2", 0), ("t1", 0))
                pe.matmul(o[0:UDIM, :], luT[:], t1_sb[:], start=True, stop=True).then_inc(made, 1)
                pe.wait_ge(silu_step, 3)
                columns(product(("scT", 0)), 0, silu_c).then_inc(made, 1)

                def modulation(k):
                    pe.wait_ge(in_mod[k // 2], 16)
                    at = (k % 2) * D
                    o = product(("mod", k), ("scT", 0))
                    times(o[0:B, :], lambda j: scT[:, j * B:(j + 1) * B],
                          lambda j: wmod_sb[k // 2][:, j, at:at + D]).then_inc(made, 1)

                for k in range(GA + 2):
                    modulation(k)
                pe.wait_ge(in_rows, 16 * len(SMALL_ROWS))
                o = product(("rep", 0))
                for n, row in enumerate((bq_r, bk_r, bv_r)):
                    last = columns(o, n * CH * B, row)
                last.then_inc(made, 1)
                o = product(("wqbk", 0), ("rep", 0))
                times(o[0:B, :], lambda j: rep_of(1, j), lambda j: wqT[:, j, :]).then_inc(made, 1)
                pe.wait_ge(in_o, 16)
                o = product(("bvo", 0))
                times(o[0:B, :], lambda j: rep_of(2, j), lambda j: wo_sb[:, j, :]).then_inc(made, 1)
                for k in range(GA + 2, KINDS):
                    modulation(k)
                o = product(("cols", 0), ("mod", KINDS - 1))
                for q, kind in enumerate((CA, SA, CB, SB)):
                    last = columns(o, q * CH * B, mod[:, kind, :])
                last.then_inc(made, 1)
                o = product(("u_bias", 0))
                for n in range(CH):
                    last = times(o[:, n:n + 1], lambda j: wkT[:, j, chunk(n)], lambda j: rep_of(0, j)[:, 0:1])
                last.then_inc(made, 1)

            @block.vector
            def _(dve):
                dve.wait_ge(e_made, 1)
                dve.tensor_scalar(silu_d[:], silu_d[:], 1.0, None, ALU.add).then_inc(silu_step, 1)
                dve.wait_ge(silu_step, 1)
                dve.reciprocal(silu_d[:], silu_d[:]).then_inc(silu_step, 1)
                dve.wait_ge(silu_step, 2)
                dve.tensor_tensor(silu_c[:], c_sb[:], silu_d[:], ALU.mult).then_inc(silu_step, 1)

                def take(key):
                    kind, n = key
                    o = bank(key)
                    if key in split:
                        dve.wait_ge(hi_made, split.index(key) + 1)
                        dve.tensor_tensor(m_w[:, LO, n, :], o[:], m_w[:, HI, n, :].bitcast(F32),
                                          ALU.subtract).then_inc(taken_v, 1)
                        return
                    dve.wait_ge(made, number[key] + 1)
                    if kind in ("wqT", "wkT", "wvT"):
                        last = dve.tensor_copy({"wqT": wqT, "wkT": wkT, "wvT": wvT}[kind][:, n, :], o[:])
                    elif kind == "upT":
                        last = dve.tensor_copy(upT[:], o[:])
                    elif kind == "t1":
                        last = dve.tensor_copy(t1_sb[:], o[0:RANK, :])
                    elif kind == "t2":
                        last = dve.tensor_copy(t2_sb[:], o[0:UDIM, :])
                    elif kind == "u_bias":
                        last = dve.tensor_copy(u_bias[:], o[:, 0:CH])
                    elif kind == "rep":
                        last = dve.tensor_copy(rep[:], o[:, 0:3 * CH * B])
                    elif kind == "wqbk":
                        last = dve.tensor_copy(wqbk[:], o[0:B, :])
                    elif kind == "bvo":
                        dve.wait_ge(in_rows, 16 * len(SMALL_ROWS))
                        last = dve.tensor_tensor(bvo[:], o[0:B, :], bo_r[:], ALU.add)
                    elif kind == "scT":
                        last = dve.tensor_copy(scT[:], o[:, 0:CH * B])
                    elif kind == "mod":
                        last = dve.tensor_scalar(mod[:, n, :], o[0:B, :], 1.0 if n in (CA, CB) else 0.0, None, ALU.add)
                    else:
                        last = dve.tensor_copy(cols[:].rearrange("p (b q) -> p b q", b=B),
                                               o[:, 0:4 * CH * B].rearrange("p (q b) -> p b q", b=B))
                    last.then_inc(taken_v, 1)

                step = [0]

                def row(ins, wait=True):
                    step[0] += 1
                    ins.then_inc(row_step, 1)
                    if wait:
                        dve.wait_ge(row_step, step[0])

                def gates(n, kind):
                    row(dve.tensor_scalar(sign[:, n, :], mod[:, kind, :], 0.0, 2.0, ALU.is_ge, ALU.mult), False)
                    row(dve.scalar_tensor_tensor(size[:, n, :], mod[:, kind, :], -1.0, mod[:, kind, :], ALU.mult,
                                                 ALU.max))
                    row(dve.tensor_scalar(size[:, n, :], size[:, n, :], GATE_MIN, None, ALU.max))
                    row(dve.scalar_tensor_tensor(gate[:, n, :], sign[:, n, :], -1.0, size[:, n, :], ALU.add,
                                                 ALU.mult))

                for key in by_vector:
                    take(key)
                    if key == ("bvo", 0):
                        dve.wait_ge(taken_v, by_vector.index(key) + 1)
                        gates(0, GA)
                        row(dve.tensor_tensor(r1[:], gate[:, 0, :], bvo[:], ALU.mult), False)
                        row(dve.tensor_tensor(z[:, 0:D], mod[:, CA, :], wqbk[:], ALU.mult), False)
                        row(dve.tensor_tensor_reduce(prod[:], bq_r[:], bk_r[:], 1.0, 0.0, ALU.mult, ALU.add, bqbk[:]))
                        row(dve.tensor_tensor_reduce(prod[:], mod[:, SA, :], wqbk[:], 1.0, bqbk[:], ALU.mult, ALU.add,
                                                     z[:, D:D + 1]), False)
                        assert step[0] == EARLY_ROWS
                    if key == ("cols", 0):
                        dve.wait_ge(taken_v, by_vector.index(key) + 1)
                        gates(1, GB)
                        row(dve.tensor_tensor(r2[:], gate[:, 1, :], b_r[:], ALU.mult), False)
                        assert step[0] == ALL_ROWS


def run(nc, env, sem):
    g = env
    B, D, CH, TPB, N, SCALE, ZW = (g[k] for k in ("B", "D", "CH", "TPB", "N", "SCALE", "ZW"))
    hT, uT, v_sb, pT, h2T, x_sb = (g[k] for k in ("hT", "uT", "v_sb", "pT", "h2T", "x_sb"))
    n1, n2, h1, h2, exp_a, exp_b, prob_a, prob = (
        g[k] for k in ("n1", "n2", "h1", "h2", "exp_a", "exp_b", "prob_a", "prob"))
    gated_y, gated_o, junk = (g[k] for k in ("gated_y", "gated_o", "junk"))
    z_row, ga_row, gb_row, r1_row, r2_row, cols1, cols2 = (
        g[k] for k in ("z_row", "ga_row", "gb_row", "r1_row", "r2_row", "cols1", "cols2"))
    bank_u, bank_v, bank_s, bank_t1, bank_t2, bank_y, bank_o = (
        g[k] for k in ("bank_u", "bank_v", "bank_s", "bank_t1", "bank_t2", "bank_y", "bank_o"))
    ident, m_w, vo_w, ff_w, u_bias, cols = (g[k] for k in ("ident", "m_w", "vo_w", "ff_w", "u_bias", "cols"))
    wvT, wo_sb, w_sb, t2_sb, upT, UDIM = (g[k] for k in ("wvT", "wo_sb", "w_sb", "t2_sb", "upT", "UDIM"))
    kap, kap_s, sums, share = (g[k] for k in ("kap", "kap_s", "sums", "share"))
    scores = bank_s[:, 0:2 * P]
    probT = bank_s[:, 2 * P:4 * P]

    LOAD, ST1, LN1, T1, U, FF2, FF1 = 11, 8, 7, 7, 3, -3, -2
    FIRST, LAST = -LOAD, N - 1 - FF2
    LOOP = XRING - LOAD
    ROUNDS = B - 1

    x_in = [sem(f"x_in{n}") for n in range(XRING)]
    x_out = [sem(f"x_out{n}") for n in range(XRING)]
    z_in, ga_in, gb_in, r1_in, r2_in = [sem(n) for n in ("z_in", "ga_in", "gb_in", "r1_in", "r2_in")]
    u_made, t1_made, s_made, v_made, pt_made, y_made, t2_made, o_made = [
        sem(f"{n}_made") for n in ("u", "t1", "s", "v", "pt", "y", "t2", "o")]
    cols1_set, cols2_set, u_hi, pt_hi, h1_made, h2_made, exp_made, v_hi = [
        sem(n) for n in ("cols1_set", "cols2_set", "u_hi", "pt_hi", "h1_made", "h2_made", "exp_made", "v_hi")]
    dve_init, u_lo, pt_lo, v_lo, h1_hi, h2_hi = [
        sem(n) for n in ("dve_init", "u_lo", "pt_lo", "v_lo", "h1_hi", "h2_hi")]
    st1_made, mv1_made, ve1_made, n1_made, kap_made, kap_scaled = [
        sem(n) for n in ("st1_made", "mv1_made", "ve1_made", "n1_made", "kap_made", "kap_scaled")]
    y_gated, x2_made, st2_made, mv2_made, ve2_made, n2_made, o_gated = [
        sem(n) for n in ("y_gated", "x2_made", "st2_made", "mv2_made", "ve2_made", "n2_made", "o_gated")]
    blk_made, win_made, maxk_made, neg_made, recip_made, weight_made, proba_made, prob_made = [
        sem(n) for n in ("blk_made", "win_made", "maxk_made", "neg_made", "recip_made", "weight_made",
                         "proba_made", "prob_made")]
    pool_init, h1_lo, h2_lo, rstd1_made, rstd2_made, r1_added, r2_added, out_made = [
        sem(n) for n in ("pool_init", "h1_lo", "h2_lo", "rstd1_made", "rstd2_made", "r1_added", "r2_added",
                         "out_made")]

    late_made, late_hi, late_lo = sem("late_made"), sem("late_hi"), sem("late_lo")
    late = [(vo_w, n) for n in range(CH)] + [(ff_w, n) for n in range(CH)]
    late_banks = [g["bank_x"], bank_o, bank_y, bank_v]

    def late_at(s):
        n = 2 * (s + T1)
        return [(k, *late[k], late_banks[k % len(late_banks)]) for k in range(n, n + 2) if 0 <= k < len(late)]

    assert 2 * (T1 - U) >= len(late)

    class Step:

        def __init__(self, s, i=None):
            self.s, self.i = s, i

        def has(self, t, end=N):
            return self.i is not None or 0 <= t < end

        def tile(self, t):
            return t if self.i is None else self.i + t

        def done(self, t):
            return self.tile(t + 1)

        def dma(self, t):
            return self.tile((t // TPB + 1) * TPB)

        def batch(self, t):
            return t // TPB if self.i is None else (self.i >> 4) + t // TPB

    assert TPB == 16

    def steps(engine, body):
        for s in range(FIRST, LOOP):
            body(Step(s))
        with engine.Fori(0, (ROUNDS - 1) * TPB + 1, TPB) as i:
            for s in range(LOOP, LOOP + TPB):
                body(Step(s, i))
        for s in range(LOOP + ROUNDS * TPB, LAST + 1):
            body(Step(s))

    def slot(t):
        at = HALF + t % RING * P
        return slice(at, at + P)

    def copies(t):
        if t % RING == 0:
            return [(slice(0, HALF), slice(HALF + RING * P, HALF + RING * P + HALF))]
        if t % RING == RING - 1:
            return [(slice(HALF, P), slice(0, HALF))]
        return []

    with nc.Block() as block:
        @block.sync
        def _(sp):
            def body(st):
                s = st.s
                def row(used, t, dst, rows, landed):
                    if t % TPB != TPB - 1 or not st.has(t + 1):
                        return
                    if t >= 0:
                        sp.wait_ge(used, st.done(t))
                    sp.dma_start(dst[:], rows[bass.ds(st.batch(t + 1), 1), :].rearrange("o d -> (o d)")
                                 .partition_broadcast(P)).then_inc(landed, 16)

                row(kap_made, s + LN1 - 1, z_row, g["z_rows"], z_in)
                row(r1_added, s + LN1 - 1, r1_row, g["r1_rows"], r1_in)
                row(y_gated, s - 2, ga_row, g["ga_rows"], ga_in)
                row(r2_added, s - 2, r2_row, g["r2_rows"], r2_in)
                row(o_gated, s + FF2 - 1, gb_row, g["gb_rows"], gb_in)
                t = s + FF2
                if st.has(t):
                    sp.wait_ge(out_made, st.done(t))
                    sp.dma_start(g["out_t"][st.tile(t)], x_sb[:, t % XRING, :]).then_inc(x_out[t % XRING], 16)
                t = s + LOAD
                if st.has(t):
                    if st.has(t - XRING):
                        sp.wait_ge(x_out[t % XRING], st.dma(t - XRING))
                    sp.dma_start(x_sb[:, t % XRING, :], g["x_t"][st.tile(t)]).then_inc(x_in[t % XRING], 16)

            steps(sp, body)
            for n in range(XRING):
                sp.wait_ge(x_out[n], 16 * B)

        @block.tensor
        def _(pe):
            def three(o, left, right, start=True, stop=True):
                pe.matmul(o, left(HI), right(HI), start=start, stop=False)
                pe.matmul(o, left(HI), right(LO), start=False, stop=False)
                return pe.matmul(o, left(LO), right(HI), start=False, stop=stop)

            def body(st):
                s = st.s
                t = s + FF2
                if st.has(t):
                    pe.wait_ge(h2_lo, st.done(t))
                    if st.has(t - 1):
                        pe.wait_ge(o_gated, st.done(t - 1))
                    for k in range(CH):
                        last = three(bank_o[:], lambda w: h2T[:, t % 2, w, k, :], lambda w: ff_w[:, w, k, :],
                                     k == 0, k == CH - 1)
                    last.then_inc(o_made, 1)
                t = s - 1
                if st.has(t):
                    pe.wait_ge(prob_made, st.done(t))
                    for k in range(2):
                        last = pe.transpose(probT[:, k * P:(k + 1) * P], prob[:, k * P:(k + 1) * P], ident[:])
                    last.then_inc(pt_made, 1)
                t = s + U
                if st.has(t):
                    grp, ch = t // GROUP, t % GROUP
                    pe.wait_ge(h1_lo, st.done(grp * GROUP + GROUP - 1))
                    if st.has(t - 1):
                        pe.wait_ge(u_lo, st.done(t - 1))
                    at = HALF + grp % 2 * GROUP * P
                    for k in range(CH):
                        last = three(bank_u[:], lambda w: m_w[:, w, k, ch * P:(ch + 1) * P],
                                     lambda w: hT[:, w, k, at:at + GROUP * P], k == 0, k == CH - 1)
                    last.then_inc(u_made, 1)
                t = s + FF1
                if st.has(t):
                    pe.wait_ge(n2_made, st.done(t))
                    if st.has(t - 1):
                        pe.wait_ge(h2_made, st.done(t - 1))
                    for k in range(CH):
                        last = pe.transpose(bank_t2[:, k * P:(k + 1) * P], n2[:, k * P:(k + 1) * P], ident[:])
                    last.then_inc(t2_made, 1)
                t = s - 1
                if st.has(t):
                    pe.wait_ge(pt_lo, st.done(t))
                    pe.wait_ge(v_lo, st.done(t + 1))
                    if st.has(t - 1):
                        pe.wait_ge(y_gated, st.done(t - 1))
                    for k in range(2):
                        last = three(bank_y[:], lambda w: pT[:, w, k * P:(k + 1) * P],
                                     lambda w: v_sb[:, (t + k) % 2, w, :], k == 0, k == 1)
                    last.then_inc(y_made, 1)
                if st.i is None:
                    for k, w, n, o in late_at(s):
                        if k >= len(late_banks):
                            pe.wait_ge(late_lo, k - len(late_banks) + 1)
                        own = slice(n * P, (n + 1) * P)
                        if w is vo_w:
                            pe.wait_ge(g["in_o"], 16)
                            for j in range(CH):
                                last = pe.matmul(o[:], wvT[:, j, own], wo_sb[:, j, :], start=(j == 0),
                                                 stop=(j == CH - 1))
                        else:
                            pe.wait_ge(g["in_w"], 16)
                            for j in range(CH):
                                pe.matmul(o[:, j * P:(j + 1) * P], w_sb[:, j, own], ident[:], start=(j == 0),
                                          stop=False)
                            last = pe.matmul(o[:], t2_sb[:, own], upT[0:UDIM, :], start=False, stop=True)
                        last.then_inc(late_made, 1)
                t = s + T1
                if st.has(t):
                    pe.wait_ge(n1_made, st.done(t))
                    if st.has(t - 1):
                        pe.wait_ge(h1_made, st.done(t - 1))
                    for k in range(CH):
                        last = pe.transpose(bank_t1[:, k * P:(k + 1) * P], n1[:, k * P:(k + 1) * P], ident[:])
                    last.then_inc(t1_made, 1)
                t = s
                if st.has(t):
                    grp = t // GROUP
                    pe.wait_ge(u_lo, st.done(grp * GROUP + GROUP - 1))
                    if t == 0 and st.i is None:
                        pe.wait_ge(pool_init, 2)
                    at = t % RING * P
                    q = t % GROUP * P
                    for k in range(CH):
                        last = three(scores, lambda w: uT[:, grp % 2, w, k, q:q + P],
                                     lambda w: hT[:, w, k, at:at + 2 * P], k == 0, k == CH - 1)
                    last.then_inc(s_made, 1)
                t = s + 1
                if st.has(t, N + 1):
                    if t == 0 and st.i is None:
                        pe.wait_ge(pool_init, 2)
                        pe.wait_ge(late_lo, len(late))
                    if st.has(t):
                        pe.wait_ge(h1_lo, st.done(t))
                    if st.has(t - 1):
                        pe.wait_ge(v_lo, st.done(t - 1))
                    at = t % RING * P
                    for k in range(CH):
                        last = three(bank_v[:], lambda w: hT[:, w, k, at:at + P], lambda w: vo_w[:, w, k, :],
                                     k == 0, k == CH - 1)
                    last.then_inc(v_made, 1)

            steps(pe, body)

        @block.scalar
        def _(act):
            def modulate(st, t, dst, src, cur, first, set_sem, made, ready, free, free_t):
                if t % TPB == 0:
                    at = st.batch(t) * (4 * CH) + first
                    act.copy(cur[:], cols[:, bass.ds(at, 2 * CH)]).then_inc(set_sem, 1)
                    act.wait_ge(set_sem, st.batch(t) + 1)
                act.wait_ge(ready, st.done(t))
                if st.has(free_t):
                    act.wait_ge(free, st.done(free_t))
                for k in range(CH):
                    last = act.activation(dst[:, k, :], src[:, k * P:(k + 1) * P], ACT.Identity,
                                          bias=cur[:, CH + k:CH + k + 1], scale=cur[:, k:k + 1])
                last.then_inc(made, 1)

            def body(st):
                s = st.s
                t = s - 1
                if st.has(t):
                    act.wait_ge(pt_made, st.done(t))
                    act.activation(pT[:, HI, :], probT, ACT.Copy).then_inc(pt_hi, 1)
                t = s + U
                if st.has(t):
                    grp, ch = t // GROUP, t % GROUP
                    act.wait_ge(u_made, st.done(t))
                    act.activation(uT[:, grp % 2, HI, ch, :], bank_u[:], ACT.Identity,
                                   bias=u_bias[:, ch:ch + 1]).then_inc(u_hi, 1)
                t = s + FF1
                if st.has(t):
                    modulate(st, t, h2, bank_t2, cols2, 2 * CH, cols2_set, h2_made, t2_made, h2_lo, t - 1)
                if st.i is None:
                    for k, w, n, o in late_at(s):
                        act.wait_ge(late_made, k + 1)
                        act.activation(w[:, HI, n, :], o[:], ACT.Copy).then_inc(late_hi, 1)
                t = s + T1
                if st.has(t):
                    modulate(st, t, h1, bank_t1, cols1, 0, cols1_set, h1_made, t1_made, h1_lo, t - 1)
                t = s
                if st.has(t):
                    act.wait_ge(neg_made, st.done(t))
                    for half in range(2):
                        rows = slice(half * HALF, (half + 1) * HALF)
                        for w, dst in enumerate((exp_a, exp_b)):
                            keys = slice((half + w) * HALF, (half + w) * HALF + P)
                            last = act.activation(dst[rows, keys], scores[rows, keys], ACT.Exp,
                                                  bias=g["neg_max"][rows, half + w:half + w + 1], scale=SCALE,
                                                  accum_out=sums[rows, w:w + 1])
                    last.then_inc(exp_made, 1)
                t = s + 1
                if st.has(t, N + 1):
                    act.wait_ge(v_made, st.done(t))
                    act.activation(v_sb[:, t % 2, HI, :], bank_v[:], ACT.Copy).then_inc(v_hi, 1)

            steps(act, body)

        @block.vector
        def _(dve):
            def low(dst, src, high, made):
                dve.tensor_tensor(dst, src, high.bitcast(F32), ALU.subtract).then_inc(made, 1)

            def variance(st, t, src, stats, mv, ve, st_made, mv_made, ve_made):
                dve.bn_stats(stats[:], src).then_inc(st_made, 1)
                dve.wait_ge(st_made, st.done(t))
                dve.memset(g["spare"][:], 0.0)
                dve.bn_aggr(mv[:], stats[:]).then_inc(mv_made, 1)
                dve.wait_ge(mv_made, st.done(t))
                dve.tensor_scalar(ve[:], mv[:, 1:2], LN_EPS, None, ALU.add).then_inc(ve_made, 1)

            def normalise(dst, src, mv, rstd, made):
                dve.tensor_scalar(dst[:], src, mv[:, 0:1], rstd[:], ALU.subtract, ALU.mult).then_inc(made, 1)

            dve.memset(exp_a[:], 0.0)
            dve.memset(exp_b[:], 0.0)
            dve.memset(share[:], 0.5).then_inc(dve_init, 1)
            dve.wait_ge(dve_init, 1)
            dve.memset(share[0:HALF, 0, 0:1], 0.0)
            dve.memset(share[0:HALF, 0, 1:2], 1.0)
            dve.memset(share[HALF:P, 2, 0:1], 1.0)
            dve.memset(share[HALF:P, 2, 1:2], 0.0).then_inc(dve_init, 1)
            dve.wait_ge(dve_init, 2)

            def body(st):
                s = st.s
                t = s + FF2
                if st.has(t):
                    dve.wait_ge(o_made, st.done(t))
                    if t % TPB == 0:
                        dve.wait_ge(gb_in, st.dma(t))
                    if st.has(t - 1):
                        dve.wait_ge(out_made, st.done(t - 1))
                    dve.tensor_tensor(gated_o[:], bank_o[:], gb_row[:], ALU.mult).then_inc(o_gated, 1)
                t = s - 1
                if st.has(t):
                    dve.wait_ge(pt_hi, st.done(t))
                    low(pT[:, LO, :], probT, pT[:, HI, :], pt_lo)
                t = s + LN1
                if st.has(t):
                    c = t % XRING
                    dve.wait_ge(rstd1_made, st.done(t))
                    if st.has(t - 1):
                        dve.wait_ge(t1_made, st.done(t - 1))
                    normalise(n1, x_sb[:, c, :], g["mv1"], g["rstd1"], n1_made)
                    dve.wait_ge(n1_made, st.done(t))
                    if t % TPB == 0:
                        dve.wait_ge(z_in, st.dma(t))
                    dve.tensor_tensor_reduce(junk[:], n1[:], z_row[:, 0:D], 1.0, z_row[:, D:D + 1], ALU.mult,
                                             ALU.add, kap[:, c:c + 1]).then_inc(kap_made, 1)
                    dve.wait_ge(kap_made, st.done(t))
                    dve.tensor_scalar(kap_s[:, c:c + 1], kap[:, c:c + 1], SCALE, None,
                                      ALU.mult).then_inc(kap_scaled, 1)
                t = s + U
                if st.has(t):
                    grp, ch = t // GROUP, t % GROUP
                    dve.wait_ge(u_hi, st.done(t))
                    dve.scalar_tensor_tensor(uT[:, grp % 2, LO, ch, :], bank_u[:], u_bias[:, ch:ch + 1],
                                             uT[:, grp % 2, HI, ch, :].bitcast(F32), ALU.add,
                                             ALU.subtract).then_inc(u_lo, 1)
                t = s + ST1
                if st.has(t):
                    dve.wait_ge(x_in[t % XRING], st.dma(t))
                    variance(st, t, x_sb[:, t % XRING, :], g["stats1"], g["mv1"], g["ve1"], st1_made, mv1_made,
                             ve1_made)
                t = s + FF1
                if st.has(t):
                    dve.wait_ge(h2_made, st.done(t))
                    dve.tensor_copy(h2T[:, t % 2, HI, :, :], h2[:]).then_inc(h2_hi, 1)
                t = s - 1
                if st.has(t):
                    dve.wait_ge(y_made, st.done(t))
                    if t % TPB == 0:
                        dve.wait_ge(ga_in, st.dma(t))
                    dve.tensor_tensor(gated_y[:], bank_y[:], ga_row[:], ALU.mult).then_inc(y_gated, 1)
                    dve.wait_ge(y_gated, st.done(t))
                    dve.wait_ge(r1_added, st.done(t))
                    xt = x_sb[:, t % XRING, :]
                    dve.tensor_tensor(xt, xt, gated_y[:], ALU.add).then_inc(x2_made, 1)
                t = s
                if st.has(t):
                    c = t % XRING
                    dve.wait_ge(s_made, st.done(t))
                    dve.reduce_max(g["blk_max"][:], scores.rearrange("p (b k) -> p b k", k=HALF),
                                   AX_X).then_inc(blk_made, 1)
                    dve.wait_ge(blk_made, st.done(t))
                    dve.tensor_tensor(g["win_max"][:], g["blk_max"][:, 0:3], g["blk_max"][:, 1:4],
                                      ALU.max).then_inc(win_made, 1)
                    dve.wait_ge(win_made, st.done(t))
                    dve.tensor_scalar(g["max_k"][:], g["win_max"][:], kap[:, c:c + 1], None,
                                      ALU.add).then_inc(maxk_made, 1)
                    dve.wait_ge(maxk_made, st.done(t))
                    dve.tensor_scalar(g["neg_max"][:], g["max_k"][:], -SCALE, kap_s[:, c:c + 1], ALU.mult,
                                      ALU.add).then_inc(neg_made, 1)
                if st.i is None:
                    for k, w, n, o in late_at(s):
                        dve.wait_ge(late_hi, k + 1)
                        low(w[:, LO, n, :], o[:], w[:, HI, n, :], late_lo)
                t = s + T1
                if st.has(t):
                    dve.wait_ge(h1_made, st.done(t))
                    if st.has(s):
                        dve.wait_ge(s_made, st.done(s))
                    for src, dst in copies(t):
                        dve.tensor_copy(hT[:, HI, :, dst], h1[:, :, src])
                    dve.tensor_copy(hT[:, HI, :, slot(t)], h1[:]).then_inc(h1_hi, 1)
                t = s - 1
                if st.has(t):
                    dve.wait_ge(x2_made, st.done(t))
                    variance(st, t, x_sb[:, t % XRING, :], g["stats2"], g["mv2"], g["ve2"], st2_made, mv2_made, ve2_made)
                t = s
                if st.has(t):
                    edge = {0: 0, TPB - 1: 2}.get(t % TPB, 1)
                    dve.wait_ge(exp_made, st.done(t))
                    dve.reciprocal(g["recips"][:], sums[:]).then_inc(recip_made, 1)
                    dve.wait_ge(recip_made, st.done(t))
                    dve.tensor_tensor(g["weights"][:], g["recips"][:], share[:, edge, :],
                                      ALU.mult).then_inc(weight_made, 1)
                    dve.wait_ge(weight_made, st.done(t))
                    dve.tensor_scalar(prob_a[:], exp_a[:], g["weights"][:, 0:1], None,
                                      ALU.mult).then_inc(proba_made, 1)
                    dve.wait_ge(proba_made, st.done(t))
                    dve.scalar_tensor_tensor(prob[:], exp_b[:], g["weights"][:, 1:2], prob_a[:], ALU.mult,
                                             ALU.add).then_inc(prob_made, 1)
                t = s - 1
                if st.has(t):
                    dve.wait_ge(rstd2_made, st.done(t))
                    if st.has(t - 1):
                        dve.wait_ge(t2_made, st.done(t - 1))
                    normalise(n2, x_sb[:, t % XRING, :], g["mv2"], g["rstd2"], n2_made)
                t = s + 1
                if st.has(t, N + 1):
                    dve.wait_ge(v_hi, st.done(t))
                    low(v_sb[:, t % 2, LO, :], bank_v[:], v_sb[:, t % 2, HI, :], v_lo)

            steps(dve, body)

        @block.gpsimd
        def _(pool):
            def low(dst, src, high):
                return pool.tensor_tensor(dst, src, high.bitcast(F32), ALU.subtract)

            def add_row(t, row, made):
                xt = x_sb[:, t % XRING, :]
                pool.tensor_tensor(xt, xt, row, ALU.add).then_inc(made, 1)

            pool.memset(g["minus_half"][:], -0.5).then_inc(pool_init, 1)
            pool.memset(hT[:, :, :, 0:HALF].bitcast(F32), 0.0).then_inc(pool_init, 1)
            pool.wait_ge(pool_init, 2)

            def body(st):
                s = st.s
                t = s + FF2
                if st.has(t):
                    pool.wait_ge(o_gated, st.done(t))
                    pool.wait_ge(r2_added, st.done(t))
                    add_row(t, gated_o[:], out_made)
                t = s + LN1
                if st.has(t):
                    pool.wait_ge(n1_made, st.done(t))
                    if t % TPB == 0:
                        pool.wait_ge(r1_in, st.dma(t))
                    add_row(t, r1_row[:], r1_added)
                t = s + ST1
                if st.has(t):
                    pool.wait_ge(ve1_made, st.done(t))
                    pool.tensor_tensor(g["rstd1"][:], g["ve1"][:], g["minus_half"][:], ALU.pow).then_inc(rstd1_made, 1)
                t = s + FF1
                if st.has(t):
                    pool.wait_ge(h2_hi, st.done(t))
                    low(h2T[:, t % 2, LO, :, :], h2[:], h2T[:, t % 2, HI, :, :]).then_inc(h2_lo, 1)
                t = s + T1
                if st.has(t):
                    pool.wait_ge(h1_hi, st.done(t))
                    for src, dst in copies(t):
                        low(hT[:, LO, :, dst], h1[:, :, src], hT[:, HI, :, dst])
                    low(hT[:, LO, :, slot(t)], h1[:], hT[:, HI, :, slot(t)]).then_inc(h1_lo, 1)
                t = s - 1
                if st.has(t):
                    pool.wait_ge(ve2_made, st.done(t))
                    pool.tensor_tensor(g["rstd2"][:], g["ve2"][:], g["minus_half"][:], ALU.pow).then_inc(rstd2_made, 1)
                t = s - 1
                if st.has(t):
                    pool.wait_ge(n2_made, st.done(t))
                    if t % TPB == 0:
                        pool.wait_ge(r2_in, st.dma(t))
                    add_row(t, r2_row[:], r2_added)

            steps(pool, body)


_INS = ['L0_attn_x', 'L0_attn_Wq', 'L0_attn_bq', 'L0_attn_Wk', 'L0_attn_bk', 'L0_attn_Wv', 'L0_attn_bv', 'L0_attn_Wo',
        'L0_attn_bo', 'L0_ffn_W', 'L0_ffn_b', 'L0_ffn_lora_down', 'L0_ffn_lora_up', 'L0_ffn_down_aux',
        'L0_ffn_up_aux', 'L0_c', 'L0_wmod']


def kernel(**inputs):
    import numpy as _np
    import concourse.bacc as _bacc
    from concourse import mybir as _mybir
    from concourse.bass_utils import run_bass_kernel_spmd as _run

    nc = _bacc.Bacc("TRN2", target_bir_lowering=False, num_devices=1)
    arrays, args = {}, []
    for name in _INS:
        a = _np.ascontiguousarray(inputs[name])
        arrays[f"in_{name}_dram"] = a
        args.append(nc.dram_tensor(f"in_{name}_dram", a.shape, _mybir.dt.from_np(a.dtype), kind="ExternalInput").ap())
    shape = inputs['L0_attn_x'].shape
    args.append(nc.dram_tensor("out_0_dram", shape, _mybir.dt.float32, kind="ExternalOutput").ap())
    adaln_block_kernel(nc, *args)
    r = _run(nc, [arrays], core_ids=[0])
    return r.results[0]["out_0_dram"]
```

```python
from contextlib import ExitStack

import concourse.bass as bass
from concourse import mybir

ALU = mybir.AluOpType
ACT = mybir.ActivationFunctionType
AX_X = mybir.AxisListType.X
F32 = mybir.dt.float32
F32R = mybir.dt.float32r
HI, LO = 0, 1

P = 128
HALF = P // 2
HEAD_DIM = 32
LN_EPS = 1e-5
GATE_MIN = 0.25

RING = 8
PRELOADED = 4
GROUP = 4
XRING = 16


def adaln_block_kernel(nc, x, Wq, bq, Wk, bk, Wv, bv, Wo, bo, W, b, lora_down, lora_up, down_aux, up_aux,
                       c, wmod, out):
    B, S, D = x.shape
    CH = D // P
    TPB = S // P
    N = B * TPB
    RANK, DDIM = lora_down.shape
    UDIM = lora_up.shape[0]
    KINDS = wmod.shape[1] // D
    SA, CA, GA, SB, CB, GB = range(KINDS)
    SCALE = float(HEAD_DIM) ** -0.5
    ZW = D + 1
    assert TPB == XRING and TPB % RING == 0 and RING == 2 * GROUP and CH * P == D

    x_t = x.rearrange("b (t p) d -> (b t) p d", p=P)
    out_t = out.rearrange("b (t p) d -> (b t) p d", p=P)

    with ExitStack() as ctx:
        def sb(name, shape, dt=F32, stack=ctx):
            return stack.enter_context(nc.sbuf_tensor(name, shape, dt))

        def sem(name):
            return ctx.enter_context(nc.semaphore(name))

        bank_u, bank_v, bank_s, bank_t1, bank_t2, bank_y, bank_o, bank_x = [
            ctx.enter_context(nc.psum_tensor(f"bank_{n}", [P, 512], F32))
            for n in ("u", "v", "s", "t1", "t2", "y", "o", "x")]

        ident = sb("ident", [P, P])
        m_w = sb("m_w", [P, 2, CH, D], F32R)
        vo_w = sb("vo_w", [P, 2, CH, D], F32R)
        ff_w = sb("ff_w", [P, 2, CH, D], F32R)
        u_bias = sb("u_bias", [P, CH])
        cols = sb("cols", [P, B * 4 * CH])
        z_rows = nc.dram_tensor("z_rows", [B, ZW], F32, kind="Internal").ap()
        ga_rows = nc.dram_tensor("ga_rows", [B, D], F32, kind="Internal").ap()
        gb_rows = nc.dram_tensor("gb_rows", [B, D], F32, kind="Internal").ap()
        r1_rows = nc.dram_tensor("r1_rows", [B, D], F32, kind="Internal").ap()
        r2_rows = nc.dram_tensor("r2_rows", [B, D], F32, kind="Internal").ap()

        x_sb = sb("x_sb", [P, XRING, D])
        x_in = [sem(f"x_in{n}") for n in range(XRING)]

        carried = ExitStack()
        wvT = sb("wvT", [P, CH, D], F32, carried)
        wo_sb = sb("wo_sb", [P, CH, D], F32, carried)
        w_sb = sb("w_sb", [P, CH, D], F32, carried)
        t2_sb = sb("t2_sb", [UDIM, D], F32, carried)
        upT = sb("upT", [P, D], F32, carried)
        in_o, in_w, rows_out = sem("in_o"), sem("in_w"), sem("rows_out")

        prepare(nc, locals(), sem)
        carried.close()

        main = ExitStack()
        with main:
            ms = lambda name, shape, dt=F32: sb(name, shape, dt, main)
            uT = ms("uT", [P, 2, 2, CH, GROUP * P], F32R)
            hT = ms("hT", [P, 2, CH, HALF + RING * P + HALF], F32R)
            v_sb = ms("v_sb", [P, 2, 2, D], F32R)
            pT = ms("pT", [P, 2, 2 * P], F32R)
            h2T = ms("h2T", [P, 2, 2, CH, P], F32R)
            n1 = ms("n1", [P, D])
            n2 = ms("n2", [P, D])
            h1 = ms("h1", [P, CH, P])
            h2 = ms("h2", [P, CH, P])
            exp_a = ms("exp_a", [P, 2 * P])
            exp_b = ms("exp_b", [P, 2 * P])
            prob_a = ms("prob_a", [P, 2 * P])
            prob = ms("prob", [P, 2 * P])
            gated_y = ms("gated_y", [P, D])
            gated_o = ms("gated_o", [P, D])
            junk = ms("junk", [P, D])
            z_row = ms("z_row", [P, ZW])
            ga_row = ms("ga_row", [P, D])
            gb_row = ms("gb_row", [P, D])
            r1_row = ms("r1_row", [P, D])
            r2_row = ms("r2_row", [P, D])
            cols1 = ms("cols1", [P, 2 * CH])
            cols2 = ms("cols2", [P, 2 * CH])
            stats1 = ms("stats1", [P, 6])
            stats2 = ms("stats2", [P, 6])
            mv1 = ms("mv1", [P, 2])
            mv2 = ms("mv2", [P, 2])
            ve1 = ms("ve1", [P, 1])
            ve2 = ms("ve2", [P, 1])
            rstd1 = ms("rstd1", [P, 1])
            rstd2 = ms("rstd2", [P, 1])
            minus_half = ms("minus_half", [P, 1])
            spare = ms("spare", [P, 1])
            kap = ms("kap", [P, XRING])
            kap_s = ms("kap_s", [P, XRING])
            blk_max = ms("blk_max", [P, 4])
            win_max = ms("win_max", [P, 3])
            max_k = ms("max_k", [P, 3])
            neg_max = ms("neg_max", [P, 3])
            sums = ms("sums", [P, 2])
            recips = ms("recips", [P, 2])
            weights = ms("weights", [P, 2])
            share = ms("share", [P, 3, 2])
            run(nc, locals(), sem)


def prepare(nc, env, sem):
    g = env
    B, D, CH, KINDS, ZW, RANK, DDIM, UDIM = (g[k] for k in ("B", "D", "CH", "KINDS", "ZW", "RANK", "DDIM", "UDIM"))
    SA, CA, GA, SB, CB, GB = range(KINDS)
    ident, m_w, u_bias, cols = (g[k] for k in ("ident", "m_w", "u_bias", "cols"))
    wvT, wo_sb, w_sb, t2_sb, upT = (g[k] for k in ("wvT", "wo_sb", "w_sb", "t2_sb", "upT"))
    in_o, in_w, rows_out, x_sb, x_in = (g[k] for k in ("in_o", "in_w", "rows_out", "x_sb", "x_in"))
    banks = [g[k] for k in ("bank_u", "bank_v", "bank_s", "bank_t1", "bank_t2", "bank_y", "bank_o", "bank_x")]
    NBANK = len(banks)

    with ExitStack() as ctx:
        def sb(name, shape, dt=F32):
            return ctx.enter_context(nc.sbuf_tensor(name, shape, dt))

        qk_sb = sb("qk_sb", [P, 2, CH, D])
        wq_sb, wk_sb = qk_sb[:, 0], qk_sb[:, 1]
        wv_sb = sb("wv_sb", [P, CH, D])
        wqT, wkT = [sb(f"{n}T", [P, CH, D]) for n in ("wq", "wk")]
        wmod_sb = [w.rearrange("p a b -> p (a b)").rearrange("p (c n) -> p c n", c=CH)
                   for w in (x_sb[:, 0:XRING // 2, :], x_sb[:, XRING // 2:XRING, :],
                             qk_sb[:].rearrange("p a c d -> p (a c) d"))]
        c_sb = sb("c_sb", [B, D])
        silu_d = sb("silu_d", [B, D])
        silu_c = sb("silu_c", [B, D])
        bqwk = silu_d
        scT = sb("scT", [P, CH * B])
        up_sb = sb("up_sb", [P, CH, P])
        down_sb = sb("down_sb", [DDIM, D])
        ldT = sb("ldT", [DDIM, RANK])
        luT = sb("luT", [RANK, UDIM])
        t1_sb = sb("t1_sb", [RANK, D])
        bq_r, bk_r, bv_r, bo_r, b_r = [sb(f"{n}_r", [B, D]) for n in ("bq", "bk", "bv", "bo", "bff")]
        rep = sb("rep", [P, 3 * CH * B])
        wqbk = sb("wqbk", [B, D])
        bvo = sb("bvo", [B, D])
        mod = sb("mod", [B, KINDS, D])
        gate = sb("gate", [B, 2, D])
        sign = sb("sign", [B, 2, D])
        size = sb("size", [B, 2, D])
        z = sb("z", [B, ZW])
        prod = sb("prod", [B, D])
        bqbk = sb("bqbk", [B, 1])
        r1 = sb("r1", [B, D])
        r2 = sb("r2", [B, D])

        in_q, in_k, in_v, in_c, in_rows, in_lora, in_mod0, in_mod1, in_mod2 = [
            sem(f"in_{n}") for n in ("q", "k", "v", "c", "rows", "lora", "mod0", "mod1", "mod2")]
        in_mod = [in_mod0, in_mod1, in_mod2]
        up_zero, id_zero, id_made = sem("up_zero"), sem("id_zero"), sem("id_made")
        e_made, silu_step, made = sem("e_made"), sem("silu_step"), sem("made")
        bvo_step = sem("bvo_step")
        hi_made, taken_v, taken_s, row_step = sem("hi_made"), sem("taken_v"), sem("taken_s"), sem("row_step")

        order = ([("wqT", n) for n in range(CH)] + [("wkT", n) for n in range(CH)]
                 + [("wvT", n) for n in range(CH)] + [("m", n) for n in range(CH)]
                 + [("scT", 0), ("rep", 0), ("rows0", 0), ("bvo", 0), ("upT", 0), ("t1", 0), ("vo", 0), ("t2", 0),
                    ("rows1", 0), ("vo", 1), ("cols", 0)])
        quads = {"rows0": (SA, CA, GA, "wqbk"), "rows1": (SB, CB, GB, "bqwk")}
        number = {key: n for n, key in enumerate(order)}
        split = [key for key in order if key[0] in ("m", "vo")]
        split_to = {"m": m_w, "vo": g["vo_w"]}
        by_scalar = [key for key in order if key[0] in ("wqT", "wkT", "wvT") and key[1] % 2 or key[0] in quads]
        by_vector = [key for key in order if key not in by_scalar]

        def taken(key):
            if key in by_scalar:
                return taken_s, by_scalar.index(key) + 1
            return taken_v, by_vector.index(key) + 1

        def bank(key):
            return banks[number[key] % NBANK]

        WARM = 24
        EARLY_ROWS, ALL_ROWS = 8, 13
        SMALL_ROWS = ((bq_r, g["bq"]), (bk_r, g["bk"]), (bv_r, g["bv"]), (bo_r, g["bo"]), (b_r, g["b"]))

        with nc.Block() as block:
            @block.sync
            def _(sp):
                by_rows = lambda w: w.rearrange("(c p) n -> p c n", p=P)
                wm = by_rows(g["wmod"])
                sp.dma_start(wq_sb, by_rows(g["Wq"])).then_inc(in_q, 16)
                sp.dma_start(wk_sb, by_rows(g["Wk"])).then_inc(in_k, 16)
                sp.dma_start(wv_sb[:], by_rows(g["Wv"])).then_inc(in_v, 16)
                sp.dma_start(wo_sb[:], by_rows(g["Wo"])).then_inc(in_o, 16)
                for n in range(3):
                    if n == 2:
                        sp.wait_ge(made, number[("wkT", CH - 1)] + 1)
                    sp.dma_start(wmod_sb[n], wm[:, :, 2 * n * D:2 * (n + 1) * D]).then_inc(in_mod[n], 16)
                sp.dma_start(w_sb[:], by_rows(g["W"])).then_inc(in_w, 16)
                sp.wait_ge(made, number[("rows0", 0)] + 1)
                for t in range(PRELOADED):
                    sp.dma_start(x_sb[:, t, :], g["x_t"][t]).then_inc(x_in[t], 16)
                sp.wait_ge(row_step, EARLY_ROWS)
                for rows, t in ((g["ga_rows"], gate[:, 0, :]), (g["r1_rows"], r1[:]), (g["z_rows"], z[:])):
                    sp.dma_start(rows, t).then_inc(rows_out, 16)
                sp.wait_ge(row_step, ALL_ROWS)
                for rows, t in ((g["gb_rows"], gate[:, 1, :]), (g["r2_rows"], r2[:])):
                    sp.dma_start(rows, t).then_inc(rows_out, 16)

            @block.scalar
            def _(act):
                act.dma_start(c_sb[:], g["c"]).then_inc(in_c, 16)
                for t, v in SMALL_ROWS:
                    act.dma_start(t[:], v.partition_broadcast(B)).then_inc(in_rows, 16)
                act.wait_ge(in_c, 16)
                nc.scalar.activation(silu_d[:], c_sb[:], ACT.Exp, scale=-1.0).then_inc(e_made, 1)
                act.wait_ge(up_zero, 1)
                with nc.allow_non_contiguous_dma(reason="small"):
                    for t, v in ((up_sb[:, :, 0:UDIM], g["up_aux"].rearrange("(c p) n -> p c n", p=P)),
                                 (down_sb[:], g["down_aux"]),
                                 (ldT[:], g["lora_down"].rearrange("r d -> d r")),
                                 (luT[:], g["lora_up"].rearrange("u r -> r u"))):
                        act.dma_start(t, v).then_inc(in_lora, 16)
                for key in order:
                    kind, n = key
                    if key in split:
                        act.wait_ge(made, number[key] + 1)
                        nc.scalar.activation(split_to[kind][:, HI, n, :], bank(key)[:], ACT.Copy).then_inc(hi_made, 1)
                    elif kind in quads:
                        act.wait_ge(made, number[key] + 1)
                        act.wait_ge(silu_step, 3)
                        for q, what in enumerate(quads[kind]):
                            dst = {"wqbk": wqbk[:], "bqwk": bqwk[:]}[what] if isinstance(what, str) else mod[:, what, :]
                            last = nc.scalar.activation(dst, bank(key)[q * 32:q * 32 + B, :], ACT.Copy,
                                                        bias=1.0 if what in (CA, CB) else 0.0)
                        last.then_inc(taken_s, 1)
                    elif key in by_scalar:
                        act.wait_ge(made, number[key] + 1)
                        dst = {"wqT": wqT, "wkT": wkT, "wvT": wvT}[kind]
                        nc.scalar.activation(dst[:, n, :], bank(key)[:], ACT.Copy).then_inc(taken_s, 1)

            @block.gpsimd
            def _(pool):
                nc.gpsimd.memset(ident[:], 0.0).then_inc(id_zero, 1)
                pool.wait_ge(id_zero, 1)
                nc.gpsimd.affine_select(out=ident[:], in_=ident[:], compare_op=ALU.not_equal, fill=1.0, base=0,
                                        pattern=[[-1, P]], channel_multiplier=1).then_inc(id_made, 1)
                nc.gpsimd.memset(up_sb[:], 0.0).then_inc(up_zero, 1)

            @block.tensor
            def _(pe):
                def product(key, *need):
                    n = number[key]
                    need = list(need) + ([order[n - NBANK]] if n >= NBANK else [])
                    for which in (taken_v, taken_s):
                        at = [v for w, v in map(taken, need) if w is which]
                        if at:
                            pe.wait_ge(which, max(at))
                    return bank(key)

                chunk = lambda n: slice(n * P, (n + 1) * P)

                def transposes(key, src):
                    o = product(key)
                    for j in range(CH):
                        last = pe.transpose(o[:, chunk(j)], src[:, j, chunk(key[1])], ident[:])
                    last.then_inc(made, 1)

                def times(o, lhs, rhs):
                    for j in range(CH):
                        last = pe.matmul(o, lhs(j), rhs(j), start=(j == 0), stop=(j == CH - 1))
                    return last

                def columns(o, at, row):
                    for j in range(CH):
                        last = pe.transpose(o[:, at + j * B:at + (j + 1) * B], row[:, chunk(j)], ident[0:B, 0:B])
                    return last

                both = lambda name: [(name, n) for n in range(CH)]
                rep_of = lambda n, j: rep[:, (n * CH + j) * B:(n * CH + j + 1) * B]
                pe.wait_ge(id_made, 1)
                for _ in range(WARM):
                    pe.transpose(g["bank_x"][:, 0:P], ident[:], ident[:])
                pe.wait_ge(in_q, 16)
                for n in range(CH):
                    transposes(("wqT", n), wq_sb)
                pe.wait_ge(in_k, 16)
                for n in range(CH):
                    transposes(("wkT", n), wk_sb)
                pe.wait_ge(in_v, 16)
                for n in range(CH):
                    transposes(("wvT", n), wv_sb)
                for n in range(CH):
                    o = product(("m", n), *both("wqT"), *both("wkT"))
                    times(o[:], lambda j: wqT[:, j, chunk(n)], lambda j: wkT[:, j, :]).then_inc(made, 1)

                def value_product(n):
                    o = product(("vo", n), *both("wvT"))
                    times(o[:], lambda j: wvT[:, j, chunk(n)], lambda j: wo_sb[:, j, :]).then_inc(made, 1)

                def value_product(n):
                    o = product(("vo", n), *both("wvT"))
                    times(o[:], lambda j: wvT[:, j, chunk(n)], lambda j: wo_sb[:, j, :]).then_inc(made, 1)

                def operands(what, j):
                    if what == "wqbk":
                        return rep_of(1, j), wqT[:, j, :]
                    if what == "bqwk":
                        return rep_of(0, j), wkT[:, j, :]
                    at = (what % 2) * D
                    return scT[:, j * B:(j + 1) * B], wmod_sb[what // 2][:, j, at:at + D]

                def quad_rows(name, *landed):
                    for which in landed:
                        pe.wait_ge(which, 16)
                    o = product((name, 0), ("scT", 0), ("rep", 0))
                    for j in range(CH):
                        for q, what in enumerate(quads[name]):
                            at = q * 32
                            left, right = operands(what, j)
                            last = pe.matmul(o[at:at + B, :], left, right, start=(j == 0), stop=(j == CH - 1))
                    last.then_inc(made, 1)

                pe.wait_ge(silu_step, 3)
                columns(product(("scT", 0)), 0, silu_c).then_inc(made, 1)
                pe.wait_ge(in_rows, 16 * len(SMALL_ROWS))
                o = product(("rep", 0))
                for n, row in enumerate((bq_r, bk_r, bv_r)):
                    last = columns(o, n * CH * B, row)
                last.then_inc(made, 1)
                quad_rows("rows0", in_mod0, in_mod1)
                pe.wait_ge(in_o, 16)
                o = product(("bvo", 0))
                for j in range(CH):
                    last = pe.matmul(o[j * 32:j * 32 + B, :], rep_of(2, j), wo_sb[:, j, :], start=True, stop=True)
                last.then_inc(made, 1)
                pe.wait_ge(in_lora, 16 * 4)
                o = product(("upT", 0))
                for j in range(CH):
                    last = pe.transpose(o[:, chunk(j)], up_sb[:, j, :], ident[:])
                last.then_inc(made, 1)
                o = product(("t1", 0))
                pe.matmul(o[0:RANK, :], ldT[:], down_sb[:], start=True, stop=True).then_inc(made, 1)
                value_product(0)
                o = product(("t2", 0), ("t1", 0))
                pe.matmul(o[0:UDIM, :], luT[:], t1_sb[:], start=True, stop=True).then_inc(made, 1)
                quad_rows("rows1", in_mod2)
                value_product(1)
                o = product(("cols", 0), ("rows1", 0))
                for q, kind in enumerate((CA, SA, CB, SB)):
                    last = columns(o, q * CH * B, mod[:, kind, :])
                last = columns(o, 4 * CH * B, bqwk)
                last.then_inc(made, 1)

            @block.vector
            def _(dve):
                def silu():
                    dve.wait_ge(e_made, 1)
                    dve.tensor_scalar(silu_d[:], silu_d[:], 1.0, None, ALU.add).then_inc(silu_step, 1)
                    dve.wait_ge(silu_step, 1)
                    dve.reciprocal(silu_d[:], silu_d[:]).then_inc(silu_step, 1)
                    dve.wait_ge(silu_step, 2)
                    dve.tensor_tensor(silu_c[:], c_sb[:], silu_d[:], ALU.mult).then_inc(silu_step, 1)
                    dve.wait_ge(silu_step, 3)

                def take(key):
                    kind, n = key
                    o = bank(key)
                    if key in split:
                        dve.wait_ge(hi_made, split.index(key) + 1)
                        w = split_to[kind]
                        dve.tensor_tensor(w[:, LO, n, :], o[:], w[:, HI, n, :].bitcast(F32),
                                          ALU.subtract).then_inc(taken_v, 1)
                        return
                    dve.wait_ge(made, number[key] + 1)
                    if kind in ("wqT", "wkT", "wvT"):
                        last = dve.tensor_copy({"wqT": wqT, "wkT": wkT, "wvT": wvT}[kind][:, n, :], o[:])
                    elif kind == "upT":
                        last = dve.tensor_copy(upT[:], o[:])
                    elif kind == "t1":
                        last = dve.tensor_copy(t1_sb[:], o[0:RANK, :])
                    elif kind == "t2":
                        last = dve.tensor_copy(t2_sb[:], o[0:UDIM, :])
                    elif kind == "rep":
                        last = dve.tensor_copy(rep[:], o[:, 0:3 * CH * B])
                    elif kind == "bvo":
                        dve.wait_ge(in_rows, 16 * len(SMALL_ROWS))
                        for j in range(CH):
                            if j > 0:
                                dve.wait_ge(bvo_step, j)
                            last = dve.tensor_tensor(bvo[:], o[j * 32:j * 32 + B, :], (bvo if j else bo_r)[:], ALU.add)
                            if j < CH - 1:
                                last.then_inc(bvo_step, 1)
                    elif kind == "scT":
                        last = dve.tensor_copy(scT[:], o[:, 0:CH * B])
                    else:
                        bias = o[:, 4 * CH * B:5 * CH * B].rearrange("p (c b) -> p c b", b=B)
                        dve.tensor_copy(u_bias[:], bias[:, :, 0])
                        last = dve.tensor_copy(cols[:].rearrange("p (b q) -> p b q", b=B),
                                               o[:, 0:4 * CH * B].rearrange("p (q b) -> p b q", b=B))
                    last.then_inc(taken_v, 1)

                step = [0]

                def row(ins, wait=True):
                    step[0] += 1
                    ins.then_inc(row_step, 1)
                    if wait:
                        dve.wait_ge(row_step, step[0])

                def gates(n, kind):
                    row(dve.tensor_scalar(sign[:, n, :], mod[:, kind, :], 0.0, 2.0, ALU.is_ge, ALU.mult), False)
                    row(dve.scalar_tensor_tensor(size[:, n, :], mod[:, kind, :], -1.0, mod[:, kind, :], ALU.mult,
                                                 ALU.max))
                    row(dve.tensor_scalar(size[:, n, :], size[:, n, :], GATE_MIN, None, ALU.max))
                    row(dve.scalar_tensor_tensor(gate[:, n, :], sign[:, n, :], -1.0, size[:, n, :], ALU.add,
                                                 ALU.mult))

                for key in by_vector:
                    if key == ("vo", 1):
                        dve.wait_ge(taken_s, by_scalar.index(("rows1", 0)) + 1)
                        gates(1, GB)
                        row(dve.tensor_tensor(r2[:], gate[:, 1, :], b_r[:], ALU.mult), False)
                        assert step[0] == ALL_ROWS
                    take(key)
                    if key == ("wvT", CH - 2):
                        silu()
                    if key == ("t2", 0):
                        dve.wait_ge(taken_v, by_vector.index(key) + 1)
                        dve.wait_ge(taken_s, by_scalar.index(("rows0", 0)) + 1)
                        gates(0, GA)
                        row(dve.tensor_tensor(r1[:], gate[:, 0, :], bvo[:], ALU.mult), False)
                        row(dve.tensor_tensor(z[:, 0:D], mod[:, CA, :], wqbk[:], ALU.mult), False)
                        row(dve.tensor_tensor_reduce(prod[:], bq_r[:], bk_r[:], 1.0, 0.0, ALU.mult, ALU.add, bqbk[:]))
                        row(dve.tensor_tensor_reduce(prod[:], mod[:, SA, :], wqbk[:], 1.0, bqbk[:], ALU.mult, ALU.add,
                                                     z[:, D:D + 1]), False)
                        assert step[0] == EARLY_ROWS


def run(nc, env, sem):
    g = env
    B, D, CH, TPB, N, SCALE, ZW = (g[k] for k in ("B", "D", "CH", "TPB", "N", "SCALE", "ZW"))
    hT, uT, v_sb, pT, h2T, x_sb = (g[k] for k in ("hT", "uT", "v_sb", "pT", "h2T", "x_sb"))
    n1, n2, h1, h2, exp_a, exp_b, prob_a, prob = (
        g[k] for k in ("n1", "n2", "h1", "h2", "exp_a", "exp_b", "prob_a", "prob"))
    gated_y, gated_o, junk = (g[k] for k in ("gated_y", "gated_o", "junk"))
    z_row, ga_row, gb_row, r1_row, r2_row, cols1, cols2 = (
        g[k] for k in ("z_row", "ga_row", "gb_row", "r1_row", "r2_row", "cols1", "cols2"))
    bank_u, bank_v, bank_s, bank_t1, bank_t2, bank_y, bank_o = (
        g[k] for k in ("bank_u", "bank_v", "bank_s", "bank_t1", "bank_t2", "bank_y", "bank_o"))
    ident, m_w, vo_w, ff_w, u_bias, cols = (g[k] for k in ("ident", "m_w", "vo_w", "ff_w", "u_bias", "cols"))
    wvT, wo_sb, w_sb, t2_sb, upT, UDIM = (g[k] for k in ("wvT", "wo_sb", "w_sb", "t2_sb", "upT", "UDIM"))
    kap, kap_s, sums, share = (g[k] for k in ("kap", "kap_s", "sums", "share"))
    u_banks = bank_u, g["bank_x"]
    scores = bank_s[:, 0:2 * P]
    probT = bank_s[:, 2 * P:4 * P]

    LOAD, ST1, LN1, T1, U, FF2, FF1 = 11, 8, 7, 7, 3, -3, -2
    FIRST, LAST = -LOAD, N - 1 - FF2
    LOOP = XRING - LOAD
    ROUNDS = B - 1

    x_in = g["x_in"]
    x_out = [sem(f"x_out{n}") for n in range(XRING)]
    z_in, ga_in, gb_in, r1_in, r2_in = [sem(n) for n in ("z_in", "ga_in", "gb_in", "r1_in", "r2_in")]
    u_made, t1_made, s_made, v_made, pt_made, y_made, t2_made, o_made = [
        sem(f"{n}_made") for n in ("u", "t1", "s", "v", "pt", "y", "t2", "o")]
    cols1_set, cols2_set, u_hi, pt_hi, h1_made, h1_hi, h2_made, h2_hi, exp_made, v_hi = [
        sem(n) for n in ("cols1_set", "cols2_set", "u_hi", "pt_hi", "h1_made", "h1_hi", "h2_made", "h2_hi",
                         "exp_made", "v_hi")]
    dve_init, u_lo, pt_lo, v_lo = [sem(n) for n in ("dve_init", "u_lo", "pt_lo", "v_lo")]
    st1_made, mv1_made, ve1_made, n1_made, kap_made, kap_scaled = [
        sem(n) for n in ("st1_made", "mv1_made", "ve1_made", "n1_made", "kap_made", "kap_scaled")]
    y_gated, x2_made, st2_made, mv2_made, ve2_made, n2_made, o_gated = [
        sem(n) for n in ("y_gated", "x2_made", "st2_made", "mv2_made", "ve2_made", "n2_made", "o_gated")]
    blk_made, win_made, maxk_made, neg_made, recip_made, weight_made, proba_made, prob_made = [
        sem(n) for n in ("blk_made", "win_made", "maxk_made", "neg_made", "recip_made", "weight_made",
                         "proba_made", "prob_made")]
    pool_init, h1_lo, h2_lo, rstd1_made, rstd2_made, r1_added, r2_added, out_made = [
        sem(n) for n in ("pool_init", "h1_lo", "h2_lo", "rstd1_made", "rstd2_made", "r1_added", "r2_added",
                         "out_made")]

    late_made, late_hi, late_lo = sem("late_made"), sem("late_hi"), sem("late_lo")
    late = [(vo_w, 2), (vo_w, 3), (ff_w, 0), (ff_w, 1), (ff_w, 2), (ff_w, 3)]
    late_first = {-T1: 0, 1 - T1: 1, 2 - T1: 2, 3 - T1: 4, 4 - T1: 5, 5 - T1: 6}
    late_banks = [bank_v, bank_o, bank_y]

    def late_at(s):
        return [(k, *late[k], late_banks[k % len(late_banks)])
                for k in range(late_first.get(s, len(late)), late_first.get(s + 1, len(late)))]

    FIRST_VALUES = 3 - T1

    class Step:

        def __init__(self, s, i=None):
            self.s, self.i = s, i

        def has(self, t, end=N):
            return self.i is not None or 0 <= t < end

        def tile(self, t):
            return t if self.i is None else self.i + t

        def done(self, t):
            return self.tile(t + 1)

        def dma(self, t):
            return self.tile((t // TPB + 1) * TPB)

        def batch(self, t):
            return t // TPB if self.i is None else (self.i >> 4) + t // TPB

    def values_at(st):
        t = st.s + 1
        if st.i is None and st.s == FIRST_VALUES:
            return [0]
        return [t] if st.has(t, N + 1) and (st.i is not None or t != 0) else []

    assert TPB == 16

    def steps(engine, body):
        for s in range(FIRST, LOOP):
            body(Step(s))
        with engine.Fori(0, (ROUNDS - 1) * TPB + 1, TPB) as i:
            for s in range(LOOP, LOOP + TPB):
                body(Step(s, i))
        for s in range(LOOP + ROUNDS * TPB, LAST + 1):
            body(Step(s))

    def slot(t):
        at = HALF + t % RING * P
        return slice(at, at + P)

    def copies(t):
        if t % RING == 0:
            return [(slice(0, HALF), slice(HALF + RING * P, HALF + RING * P + HALF))]
        if t % RING == RING - 1:
            return [(slice(HALF, P), slice(0, HALF))]
        return []

    with nc.Block() as block:
        @block.sync
        def _(sp):
            def body(st):
                s = st.s
                def row(used, t, dst, rows, landed):
                    if t % TPB != TPB - 1 or not st.has(t + 1):
                        return
                    if t >= 0:
                        sp.wait_ge(used, st.done(t))
                    else:
                        sp.wait_ge(g["rows_out"], 16 * 5)
                    sp.dma_start(dst[:], rows[bass.ds(st.batch(t + 1), 1), :].rearrange("o d -> (o d)")
                                 .partition_broadcast(P)).then_inc(landed, 16)

                row(kap_made, s + LN1 - 1, z_row, g["z_rows"], z_in)
                row(r1_added, s + LN1 - 1, r1_row, g["r1_rows"], r1_in)
                row(y_gated, s - 2, ga_row, g["ga_rows"], ga_in)
                row(r2_added, s - 2, r2_row, g["r2_rows"], r2_in)
                row(o_gated, s + FF2 - 1, gb_row, g["gb_rows"], gb_in)
                t = s + FF2
                if st.has(t):
                    sp.wait_ge(out_made, st.done(t))
                    sp.dma_start(g["out_t"][st.tile(t)], x_sb[:, t % XRING, :]).then_inc(x_out[t % XRING], 16)
                t = s + LOAD
                if st.has(t) and (st.i is not None or t >= PRELOADED):
                    if st.has(t - XRING):
                        sp.wait_ge(x_out[t % XRING], st.dma(t - XRING))
                    sp.dma_start(x_sb[:, t % XRING, :], g["x_t"][st.tile(t)]).then_inc(x_in[t % XRING], 16)

            steps(sp, body)
            for n in range(XRING):
                sp.wait_ge(x_out[n], 16 * B)

        @block.tensor
        def _(pe):
            def three(o, left, right, start=True, stop=True):
                pe.matmul(o, left(HI), right(HI), start=start, stop=False)
                pe.matmul(o, left(HI), right(LO), start=False, stop=False)
                return pe.matmul(o, left(LO), right(HI), start=False, stop=stop)

            def project(t, chunks):
                own, at = t % GROUP * P, HALF + t // GROUP % 2 * GROUP * P
                for k in chunks:
                    last = three(u_banks[t % 2][:], lambda w: m_w[:, w, k, own:own + P],
                                 lambda w: hT[:, w, k, at:at + GROUP * P], k == 0, k == CH - 1)
                return last

            def body(st):
                s = st.s
                t = s + FF2
                if st.has(t):
                    pe.wait_ge(h2_lo, st.done(t))
                    if st.has(t - 1):
                        pe.wait_ge(o_gated, st.done(t - 1))
                    for k in range(CH):
                        last = three(bank_o[:], lambda w: h2T[:, t % 2, w, k, :], lambda w: ff_w[:, w, k, :],
                                     k == 0, k == CH - 1)
                    last.then_inc(o_made, 1)
                if st.i is None:
                    for k, w, n, o in late_at(s):
                        own = slice(n * P, (n + 1) * P)
                        if k >= len(late_banks):
                            pe.wait_ge(late_lo, k - len(late_banks) + 1)
                        if w is vo_w:
                            for j in range(CH):
                                last = pe.matmul(o[:], wvT[:, j, own], wo_sb[:, j, :], start=(j == 0),
                                                 stop=(j == CH - 1))
                        else:
                            pe.wait_ge(g["in_w"], 16)
                            for j in range(CH):
                                pe.matmul(o[:, j * P:(j + 1) * P], w_sb[:, j, own], ident[:], start=(j == 0),
                                          stop=False)
                            last = pe.matmul(o[:], t2_sb[:, own], upT[0:UDIM, :], start=False, stop=True)
                        last.then_inc(late_made, 1)
                t = s + U
                if st.has(t):
                    pe.wait_ge(h1_lo, st.done(t // GROUP * GROUP + GROUP - 1))
                    if st.has(t - 2):
                        pe.wait_ge(u_lo, st.done(t - 2))
                    project(t, range(0, CH // 2))
                t = s - 1
                if st.has(t):
                    pe.wait_ge(prob_made, st.done(t))
                    for k in range(2):
                        last = pe.transpose(probT[:, k * P:(k + 1) * P], prob[:, k * P:(k + 1) * P], ident[:])
                    last.then_inc(pt_made, 1)
                t = s + U
                if st.has(t):
                    project(t, range(CH // 2, CH)).then_inc(u_made, 1)
                t = s + FF1
                if st.has(t):
                    pe.wait_ge(n2_made, st.done(t))
                    if st.has(t - 1):
                        pe.wait_ge(h2_made, st.done(t - 1))
                    for k in range(CH):
                        last = pe.transpose(bank_t2[:, k * P:(k + 1) * P], n2[:, k * P:(k + 1) * P], ident[:])
                    last.then_inc(t2_made, 1)
                t = s - 1
                if st.has(t):
                    pe.wait_ge(pt_lo, st.done(t))
                    pe.wait_ge(v_lo, st.done(t + 1))
                    if t == 0 and st.i is None:
                        pe.wait_ge(late_lo, len(late))
                    if st.has(t - 1):
                        pe.wait_ge(y_gated, st.done(t - 1))
                    for k in range(2):
                        last = three(bank_y[:], lambda w: pT[:, w, k * P:(k + 1) * P],
                                     lambda w: v_sb[:, (t + k) % 2, w, :], k == 0, k == 1)
                    last.then_inc(y_made, 1)
                t = s + T1
                if st.has(t):
                    pe.wait_ge(n1_made, st.done(t))
                    if st.has(t - 1):
                        pe.wait_ge(h1_made, st.done(t - 1))
                    for k in range(CH):
                        last = pe.transpose(bank_t1[:, k * P:(k + 1) * P], n1[:, k * P:(k + 1) * P], ident[:])
                    last.then_inc(t1_made, 1)
                t = s
                if st.has(t):
                    grp = t // GROUP
                    pe.wait_ge(u_lo, st.done(grp * GROUP + GROUP - 1))
                    if t == 0 and st.i is None:
                        pe.wait_ge(pool_init, 2)
                    at = t % RING * P
                    q = t % GROUP * P
                    for k in range(CH):
                        last = three(scores, lambda w: uT[:, grp % 2, w, k, q:q + P],
                                     lambda w: hT[:, w, k, at:at + 2 * P], k == 0, k == CH - 1)
                    last.then_inc(s_made, 1)
                for t in values_at(st):
                    if t == 0 and st.i is None:
                        pe.wait_ge(pool_init, 2)
                        pe.wait_ge(late_lo, 4)
                    if st.has(t):
                        pe.wait_ge(h1_lo, st.done(t))
                    if st.has(t - 1):
                        pe.wait_ge(v_lo, st.done(t - 1))
                    at = t % RING * P
                    for k in range(CH):
                        last = three(bank_v[:], lambda w: hT[:, w, k, at:at + P], lambda w: vo_w[:, w, k, :],
                                     k == 0, k == CH - 1)
                    last.then_inc(v_made, 1)

            steps(pe, body)

        @block.scalar
        def _(act):
            def modulate(st, t, dst, src, cur, first, set_sem, made, ready, free, free_t):
                if t % TPB == 0:
                    at = st.batch(t) * (4 * CH) + first
                    act.copy(cur[:], cols[:, bass.ds(at, 2 * CH)]).then_inc(set_sem, 1)
                    act.wait_ge(set_sem, st.batch(t) + 1)
                act.wait_ge(ready, st.done(t))
                if st.has(free_t):
                    act.wait_ge(free, st.done(free_t))
                for k in range(CH):
                    last = act.activation(dst[:, k, :], src[:, k * P:(k + 1) * P], ACT.Identity,
                                          bias=cur[:, CH + k:CH + k + 1], scale=cur[:, k:k + 1])
                last.then_inc(made, 1)

            def body(st):
                s = st.s
                t = s - 1
                if st.has(t):
                    act.wait_ge(pt_made, st.done(t))
                    act.activation(pT[:, HI, :], probT, ACT.Copy).then_inc(pt_hi, 1)
                t = s + U
                if st.has(t):
                    grp, ch = t // GROUP, t % GROUP
                    act.wait_ge(u_made, st.done(t))
                    act.activation(uT[:, grp % 2, HI, ch, :], u_banks[t % 2][:], ACT.Identity,
                                   bias=u_bias[:, ch:ch + 1]).then_inc(u_hi, 1)
                t = s + FF1
                if st.has(t):
                    modulate(st, t, h2, bank_t2, cols2, 2 * CH, cols2_set, h2_made, t2_made, h2_lo, t - 1)
                    act.wait_ge(h2_made, st.done(t))
                    act.activation(h2T[:, t % 2, HI, :, :], h2[:], ACT.Copy).then_inc(h2_hi, 1)
                if st.i is None:
                    for k, w, n, o in late_at(s):
                        act.wait_ge(late_made, k + 1)
                        act.activation(w[:, HI, n, :], o[:], ACT.Copy).then_inc(late_hi, 1)
                t = s + T1
                if st.has(t):
                    modulate(st, t, h1, bank_t1, cols1, 0, cols1_set, h1_made, t1_made, h1_lo, t - 1)
                    act.wait_ge(h1_made, st.done(t))
                    if st.has(s):
                        act.wait_ge(s_made, st.done(s))
                    for src, dst in copies(t):
                        act.activation(hT[:, HI, :, dst], h1[:, :, src], ACT.Copy)
                    act.activation(hT[:, HI, :, slot(t)], h1[:], ACT.Copy).then_inc(h1_hi, 1)
                t = s
                if st.has(t):
                    act.wait_ge(neg_made, st.done(t))
                    for half in range(2):
                        rows = slice(half * HALF, (half + 1) * HALF)
                        for w, dst in enumerate((exp_a, exp_b)):
                            keys = slice((half + w) * HALF, (half + w) * HALF + P)
                            last = act.activation(dst[rows, keys], scores[rows, keys], ACT.Exp,
                                                  bias=g["neg_max"][rows, half + w:half + w + 1], scale=SCALE,
                                                  accum_out=sums[rows, w:w + 1])
                    last.then_inc(exp_made, 1)
                for t in values_at(st):
                    act.wait_ge(v_made, st.done(t))
                    act.activation(v_sb[:, t % 2, HI, :], bank_v[:], ACT.Copy).then_inc(v_hi, 1)

            steps(act, body)

        @block.vector
        def _(dve):
            def low(dst, src, high, made):
                dve.tensor_tensor(dst, src, high.bitcast(F32), ALU.subtract).then_inc(made, 1)

            def variance(st, t, src, stats, mv, ve, st_made, mv_made, ve_made):
                dve.bn_stats(stats[:], src).then_inc(st_made, 1)
                dve.wait_ge(st_made, st.done(t))
                dve.memset(g["spare"][:], 0.0)
                dve.bn_aggr(mv[:], stats[:]).then_inc(mv_made, 1)
                dve.wait_ge(mv_made, st.done(t))
                dve.tensor_scalar(ve[:], mv[:, 1:2], LN_EPS, None, ALU.add).then_inc(ve_made, 1)

            def normalise(dst, src, mv, rstd, made):
                dve.tensor_scalar(dst[:], src, mv[:, 0:1], rstd[:], ALU.subtract, ALU.mult).then_inc(made, 1)

            def body(st):
                s = st.s
                t = s + FF2
                if st.has(t):
                    dve.wait_ge(o_made, st.done(t))
                    if t % TPB == 0:
                        dve.wait_ge(gb_in, st.dma(t))
                    if st.has(t - 1):
                        dve.wait_ge(out_made, st.done(t - 1))
                    dve.tensor_tensor(gated_o[:], bank_o[:], gb_row[:], ALU.mult).then_inc(o_gated, 1)
                t = s - 1
                if st.has(t):
                    dve.wait_ge(pt_hi, st.done(t))
                    low(pT[:, LO, :], probT, pT[:, HI, :], pt_lo)
                t = s + LN1
                if st.has(t):
                    c = t % XRING
                    dve.wait_ge(rstd1_made, st.done(t))
                    if st.has(t - 1):
                        dve.wait_ge(t1_made, st.done(t - 1))
                    normalise(n1, x_sb[:, c, :], g["mv1"], g["rstd1"], n1_made)
                    dve.wait_ge(n1_made, st.done(t))
                    if t % TPB == 0:
                        dve.wait_ge(z_in, st.dma(t))
                    dve.tensor_tensor_reduce(junk[:], n1[:], z_row[:, 0:D], 1.0, z_row[:, D:D + 1], ALU.mult,
                                             ALU.add, kap[:, c:c + 1]).then_inc(kap_made, 1)
                    dve.wait_ge(kap_made, st.done(t))
                    dve.tensor_scalar(kap_s[:, c:c + 1], kap[:, c:c + 1], SCALE, None,
                                      ALU.mult).then_inc(kap_scaled, 1)
                t = s + U
                if st.has(t):
                    grp, ch = t // GROUP, t % GROUP
                    dve.wait_ge(u_hi, st.done(t))
                    dve.scalar_tensor_tensor(uT[:, grp % 2, LO, ch, :], u_banks[t % 2][:], u_bias[:, ch:ch + 1],
                                             uT[:, grp % 2, HI, ch, :].bitcast(F32), ALU.add,
                                             ALU.subtract).then_inc(u_lo, 1)
                t = s + ST1
                if st.has(t):
                    dve.wait_ge(x_in[t % XRING], st.dma(t))
                    variance(st, t, x_sb[:, t % XRING, :], g["stats1"], g["mv1"], g["ve1"], st1_made, mv1_made,
                             ve1_made)
                t = s - 1
                if st.has(t):
                    dve.wait_ge(y_made, st.done(t))
                    if t % TPB == 0:
                        dve.wait_ge(ga_in, st.dma(t))
                    dve.tensor_tensor(gated_y[:], bank_y[:], ga_row[:], ALU.mult).then_inc(y_gated, 1)
                    dve.wait_ge(y_gated, st.done(t))
                    dve.wait_ge(r1_added, st.done(t))
                    xt = x_sb[:, t % XRING, :]
                    dve.tensor_tensor(xt, xt, gated_y[:], ALU.add).then_inc(x2_made, 1)
                t = s
                if st.has(t):
                    c = t % XRING
                    dve.wait_ge(s_made, st.done(t))
                    dve.reduce_max(g["blk_max"][:], scores.rearrange("p (b k) -> p b k", k=HALF),
                                   AX_X).then_inc(blk_made, 1)
                    dve.wait_ge(blk_made, st.done(t))
                    dve.tensor_tensor(g["win_max"][:], g["blk_max"][:, 0:3], g["blk_max"][:, 1:4],
                                      ALU.max).then_inc(win_made, 1)
                    dve.wait_ge(win_made, st.done(t))
                    dve.tensor_scalar(g["max_k"][:], g["win_max"][:], kap[:, c:c + 1], None,
                                      ALU.add).then_inc(maxk_made, 1)
                    dve.wait_ge(maxk_made, st.done(t))
                    dve.tensor_scalar(g["neg_max"][:], g["max_k"][:], -SCALE, kap_s[:, c:c + 1], ALU.mult,
                                      ALU.add).then_inc(neg_made, 1)
                if st.i is None and s == FIRST_VALUES:
                    dve.memset(exp_a[:], 0.0)
                    dve.memset(exp_b[:], 0.0)
                    dve.memset(share[:], 0.5).then_inc(dve_init, 1)
                    dve.wait_ge(dve_init, 1)
                    dve.memset(share[0:HALF, 0, 0:1], 0.0)
                    dve.memset(share[0:HALF, 0, 1:2], 1.0)
                    dve.memset(share[HALF:P, 2, 0:1], 1.0)
                    dve.memset(share[HALF:P, 2, 1:2], 0.0).then_inc(dve_init, 1)
                    dve.wait_ge(dve_init, 2)
                if st.i is None:
                    for k, w, n, o in late_at(s):
                        dve.wait_ge(late_hi, k + 1)
                        low(w[:, LO, n, :], o[:], w[:, HI, n, :], late_lo)
                t = s - 1
                if st.has(t):
                    dve.wait_ge(x2_made, st.done(t))
                    variance(st, t, x_sb[:, t % XRING, :], g["stats2"], g["mv2"], g["ve2"], st2_made, mv2_made,
                             ve2_made)
                t = s
                if st.has(t):
                    edge = {0: 0, TPB - 1: 2}.get(t % TPB, 1)
                    dve.wait_ge(exp_made, st.done(t))
                    dve.reciprocal(g["recips"][:], sums[:]).then_inc(recip_made, 1)
                    dve.wait_ge(recip_made, st.done(t))
                    dve.tensor_tensor(g["weights"][:], g["recips"][:], share[:, edge, :],
                                      ALU.mult).then_inc(weight_made, 1)
                    dve.wait_ge(weight_made, st.done(t))
                    dve.tensor_scalar(prob_a[:], exp_a[:], g["weights"][:, 0:1], None,
                                      ALU.mult).then_inc(proba_made, 1)
                    dve.wait_ge(proba_made, st.done(t))
                    dve.scalar_tensor_tensor(prob[:], exp_b[:], g["weights"][:, 1:2], prob_a[:], ALU.mult,
                                             ALU.add).then_inc(prob_made, 1)
                t = s - 1
                if st.has(t):
                    dve.wait_ge(rstd2_made, st.done(t))
                    if st.has(t - 1):
                        dve.wait_ge(t2_made, st.done(t - 1))
                    normalise(n2, x_sb[:, t % XRING, :], g["mv2"], g["rstd2"], n2_made)
                for t in values_at(st):
                    dve.wait_ge(v_hi, st.done(t))
                    low(v_sb[:, t % 2, LO, :], bank_v[:], v_sb[:, t % 2, HI, :], v_lo)

            steps(dve, body)

        @block.gpsimd
        def _(pool):
            def low(dst, src, high):
                return pool.tensor_tensor(dst, src, high.bitcast(F32), ALU.subtract)

            def add_row(t, row, made):
                xt = x_sb[:, t % XRING, :]
                pool.tensor_tensor(xt, xt, row, ALU.add).then_inc(made, 1)

            pool.memset(g["minus_half"][:], -0.5).then_inc(pool_init, 1)
            pool.memset(hT[:, :, :, 0:HALF].bitcast(F32), 0.0).then_inc(pool_init, 1)
            pool.wait_ge(pool_init, 2)

            def body(st):
                s = st.s
                t = s + FF2
                if st.has(t):
                    pool.wait_ge(o_gated, st.done(t))
                    pool.wait_ge(r2_added, st.done(t))
                    add_row(t, gated_o[:], out_made)
                t = s + LN1
                if st.has(t):
                    pool.wait_ge(n1_made, st.done(t))
                    if t % TPB == 0:
                        pool.wait_ge(r1_in, st.dma(t))
                    add_row(t, r1_row[:], r1_added)
                t = s + ST1
                if st.has(t):
                    pool.wait_ge(ve1_made, st.done(t))
                    pool.tensor_tensor(g["rstd1"][:], g["ve1"][:], g["minus_half"][:], ALU.pow).then_inc(rstd1_made, 1)
                t = s + FF1
                if st.has(t):
                    pool.wait_ge(h2_hi, st.done(t))
                    low(h2T[:, t % 2, LO, :, :], h2[:], h2T[:, t % 2, HI, :, :]).then_inc(h2_lo, 1)
                t = s + T1
                if st.has(t):
                    pool.wait_ge(h1_hi, st.done(t))
                    for src, dst in copies(t):
                        low(hT[:, LO, :, dst], h1[:, :, src], hT[:, HI, :, dst])
                    low(hT[:, LO, :, slot(t)], h1[:], hT[:, HI, :, slot(t)]).then_inc(h1_lo, 1)
                t = s - 1
                if st.has(t):
                    pool.wait_ge(ve2_made, st.done(t))
                    pool.tensor_tensor(g["rstd2"][:], g["ve2"][:], g["minus_half"][:], ALU.pow).then_inc(rstd2_made, 1)
                t = s - 1
                if st.has(t):
                    pool.wait_ge(n2_made, st.done(t))
                    if t % TPB == 0:
                        pool.wait_ge(r2_in, st.dma(t))
                    add_row(t, r2_row[:], r2_added)

            steps(pool, body)


_INS = ['L0_attn_x', 'L0_attn_Wq', 'L0_attn_bq', 'L0_attn_Wk', 'L0_attn_bk', 'L0_attn_Wv', 'L0_attn_bv', 'L0_attn_Wo',
        'L0_attn_bo', 'L0_ffn_W', 'L0_ffn_b', 'L0_ffn_lora_down', 'L0_ffn_lora_up', 'L0_ffn_down_aux',
        'L0_ffn_up_aux', 'L0_c', 'L0_wmod']


def kernel(**inputs):
    import numpy as _np
    import concourse.bacc as _bacc
    from concourse import mybir as _mybir
    from concourse.bass_utils import run_bass_kernel_spmd as _run

    nc = _bacc.Bacc("TRN2", target_bir_lowering=False, num_devices=1)
    arrays, args = {}, []
    for name in _INS:
        a = _np.ascontiguousarray(inputs[name])
        arrays[f"in_{name}_dram"] = a
        args.append(nc.dram_tensor(f"in_{name}_dram", a.shape, _mybir.dt.from_np(a.dtype), kind="ExternalInput").ap())
    shape = inputs['L0_attn_x'].shape
    args.append(nc.dram_tensor("out_0_dram", shape, _mybir.dt.float32, kind="ExternalOutput").ap())
    adaln_block_kernel(nc, *args)
    r = _run(nc, [arrays], core_ids=[0])
    return r.results[0]["out_0_dram"]
```
